# Optimizing a Trainium2 kernel written in Bass

```python
import numpy as np
import jax
import jax.numpy as jnp

def _softmax(x, axis=-1):
    return jax.nn.softmax(x, axis=axis)

def _gelu(x):
    return jax.nn.gelu(x, approximate=True)

def _silu(x):
    return jax.nn.silu(x)

def _sigmoid(x):
    return jax.nn.sigmoid(x)

def _layernorm(x, axis=-1, eps=1e-05):
    m = jnp.mean(x, axis=axis, keepdims=True)
    v = jnp.var(x, axis=axis, keepdims=True)
    return (x - m) / jnp.sqrt(v + eps)

def _scatter_add(tgt, idx, src, axis=0):
    return tgt.at[idx].add(src)

def _segment_sum(src, seg, n):
    return jax.ops.segment_sum(src, seg, n)
kernel_name = 'mk_seq_postln_d1_jaxref_r4_feef26'

def setup_inputs(seed: int=0):
    np.random.seed(seed)
    _w = jnp.asarray

    def _L0_attn_setup():
        import jax, jax.numpy as jnp
        import numpy as np
        B, N, C = (8, 1024, 256)
        key = jax.random.key(seed)
        k1, k2, k3 = jax.random.split(key, 3)
        x = jax.random.normal(k1, (B, N, C), dtype=jnp.float32)
        w_qkv = jax.random.normal(k2, (3 * C, C), dtype=jnp.float32) * C ** (-0.5)
        w_conv1 = jax.random.normal(k3, (C,), dtype=jnp.float32) * C ** (-0.5)
        return {'x': x, 'w_qkv': w_qkv, 'w_conv1': w_conv1}
    _L0_attn_in = _L0_attn_setup()

    def _L0_ffn_setup():
        import jax, jax.numpy as jnp
        import numpy as np
        D = 256
        H = 192
        E = 8
        K = 2
        NS = 2
        ROUTE_SCALE = 1.0

        def _gated_mlp(x, w1, w2):
            h = x @ w1.T
            y, g = jnp.split(h, 2, axis=-1)
            return y * jax.nn.silu(g) @ w2.T
        key = jax.random.key(seed)
        ks = jax.random.split(key, 6)
        s = 0.02
        return {'x': jax.random.normal(ks[0], (2, 256, D), jnp.float32), 'gate_w': jax.random.normal(ks[1], (E, D), jnp.float32) * s, 'W1': jax.random.normal(ks[2], (E, 2 * H, D), jnp.float32) * s, 'W2': jax.random.normal(ks[3], (E, D, H), jnp.float32) * s, 'Ws1': jax.random.normal(ks[4], (2 * NS * H, D), jnp.float32) * s, 'Ws2': jax.random.normal(ks[5], (D, NS * H), jnp.float32) * s}
    _L0_ffn_in = _L0_ffn_setup()
    _d = {'L0_attn_x': _L0_attn_in['x'], 'L0_attn_w_qkv': _L0_attn_in['w_qkv'], 'L0_attn_w_conv1': _L0_attn_in['w_conv1'], 'L0_ffn_gate_w': _L0_ffn_in['gate_w'], 'L0_ffn_W1': _L0_ffn_in['W1'], 'L0_ffn_W2': _L0_ffn_in['W2'], 'L0_ffn_Ws1': _L0_ffn_in['Ws1'], 'L0_ffn_Ws2': _L0_ffn_in['Ws2']}
    _x0 = _d['L0_attn_x']
    _d['L0_attn_x'] = jax.random.normal(jax.random.fold_in(jax.random.key(seed), 1), (2, 2048, 256), dtype=_x0.dtype)
    del _x0
    return _d

def reference(L0_attn_x, L0_attn_w_qkv, L0_attn_w_conv1, L0_ffn_gate_w, L0_ffn_W1, L0_ffn_W2, L0_ffn_Ws1, L0_ffn_Ws2):

    def _L0_attn_ref(x, w_qkv, w_conv1):
        import jax, jax.numpy as jnp
        import numpy as np
        B, N, C = (8, 1024, 256)
        b, n, c = x.shape
        scale = c ** (-0.5)
        qkv = jnp.einsum('bnc,dc->bnd', x, w_qkv)
        q = qkv[..., :c]
        k = qkv[..., c:2 * c]
        v = qkv[..., 2 * c:]
        agent = jnp.einsum('bnc,c->bn', q, w_conv1)
        agent_attn = jax.nn.softmax(jnp.einsum('bn,bnc->bc', agent * scale, k), axis=-1)
        agent_v = jax.nn.softmax(jnp.einsum('bc,bnc->bn', agent_attn, v), axis=-1)
        agent_v = jnp.einsum('bn,bnc->bc', agent_v, v)
        agent_tok = jax.nn.softmax(agent[:, :, None], axis=-1)
        return agent_tok * agent_v[:, None, :]

    def _L0_ffn_ref(x, gate_w, W1, W2, Ws1, Ws2):
        import jax, jax.numpy as jnp
        import numpy as np
        D = 256
        H = 192
        E = 8
        K = 2
        NS = 2
        ROUTE_SCALE = 1.0

        def _gated_mlp(x, w1, w2):
            h = x @ w1.T
            y, g = jnp.split(h, 2, axis=-1)
            return y * jax.nn.silu(g) @ w2.T
        x_shape = x.shape
        xf = x.reshape(-1, D)
        T = xf.shape[0]
        scores = jax.nn.softmax((xf @ gate_w.T).astype(jnp.float32), axis=-1)
        top_vals, top_idx = jax.lax.top_k(scores, K)
        weights = (top_vals * ROUTE_SCALE).astype(x.dtype)
        w_dense = jnp.zeros((T, E), x.dtype).at[jnp.arange(T)[:, None], top_idx].set(weights)
        h = jnp.einsum('td,ehd->teh', xf, W1)
        y, g = jnp.split(h, 2, axis=-1)
        eo = jnp.einsum('teh,edh->ted', y * jax.nn.silu(g), W2)
        z = jnp.einsum('te,ted->td', w_dense, eo)
        z = z + _gated_mlp(xf, Ws1, Ws2)
        return z.reshape(x_shape)
    x = L0_attn_x
    x = _layernorm(x + _L0_attn_ref(x, L0_attn_w_qkv, L0_attn_w_conv1), axis=-1)
    x = _layernorm(x + _L0_ffn_ref(x, L0_ffn_gate_w, L0_ffn_W1, L0_ffn_W2, L0_ffn_Ws1, L0_ffn_Ws2), axis=-1)
    return x

_drawn_inputs = setup_inputs


def setup_inputs(seed=0):
    import zlib

    import numpy as np

    out = dict(_drawn_inputs(seed))
    spreads = {}
    factors = {'L0_ffn_gate_w': 8.0,
     'L0_ffn_W1': 8.0,
     'L0_ffn_W2': 8.0,
     'L0_ffn_Ws1': 2.875,
     'L0_ffn_Ws2': 2.794}
    for name, (base, spread) in spreads.items():
        noise = np.random.default_rng([zlib.crc32(name.encode()), seed]).standard_normal(out[name].shape)
        drawn = base * np.exp(spread * noise) if base else spread * noise
        out[name] = jnp.asarray(drawn.astype(out[name].dtype))
    for name, factor in factors.items():
        out[name] = (out[name] * factor).astype(out[name].dtype)
    return out
```

```python
from contextlib import ExitStack

import numpy as np
import concourse.bass as bass
import concourse.mybir as mybir

F32 = mybir.dt.float32
F32R = mybir.dt.float32r
I32 = mybir.dt.int32
ALU = mybir.AluOpType
ACT = mybir.ActivationFunctionType
AX = mybir.AxisListType
RMAX = bass.bass_isa.ReduceOp.max
RADD = bass.bass_isa.ReduceOp.add

P = 128
B, N, C = 2, 2048, 256
TB = N // P
NT = B * TB
KC = C // P
E, K, H = 8, 2, 192
F = 2 * H
HS = 384
MC = HS // P
G = 4
GT = G * P
NG = NT // G
NP = NG // 2
EPS = 1e-5
SCALE = float(C) ** -0.5
CAP = B * N + P
BLOCKS = (K * B * N + E * (P - 1)) // P
NBP = (BLOCKS + 1) // 2
NBK = 2 * NBP
IDLE = 8
ROWS = E * CAP + IDLE * P
HR = H - P


def post_norm_layer(nc, x, w_qkv, w_kv_t, w_conv, gate_t, w1_t, w2_t, ws1_t, ws2_t, out):
    rows_in = nc.dram_tensor("rows_in", [ROWS, C], F32, kind="Internal").ap()
    rows_out = nc.dram_tensor("rows_out", [NBK * P, C], F32, kind="Internal").ap()

    with ExitStack() as ctx:
        def sb(name, shape, dt=F32):
            return ctx.enter_context(nc.sbuf_tensor(name, shape, dt))

        def sem(name):
            return ctx.enter_context(nc.semaphore(name))

        def pair(name):
            return [sem(f"{name}_even"), sem(f"{name}_odd")]

        xs = sb("xs", [P, NT, C])
        w1hi, w1lo = (sb(f"w1{n}", [P, E, KC, F], F32R) for n in ("hi", "lo"))
        w2hi, w2lo = (sb(f"w2{n}", [P, E, C], F32R) for n in ("hi", "lo"))
        w2rhi, w2rlo = (sb(f"w2r{n}", [P, E, C], F32R) for n in ("hi", "lo"))
        ws1hi, ws1lo = (sb(f"ws1{n}", [P, KC, 2 * HS], F32R) for n in ("hi", "lo"))
        ws2hi, ws2lo = (sb(f"ws2{n}", [P, MC, C], F32R) for n in ("hi", "lo"))
        x2 = [sb(f"x2_{n}", [P, G, C]) for n in range(2)]
        xthi, xtlo = (sb(f"xt{n}", [P, KC, GT], F32R) for n in ("hi", "lo"))
        hthi, htlo = (sb(f"ht{n}", [P, MC, GT], F32R) for n in ("hi", "lo"))
        mix = sb("mix", [P, 4, GT])
        stage = sb("stage", [P, 2, 3072])
        bxhi, bxlo = ([sb(f"bx{n}{i}", [P, KC, P], F32R) for i in range(2)] for n in ("hi", "lo"))
        bhhi = [sb(f"bhhi{i}", [P, 2, P], F32R) for i in range(2)]
        bhlo = [sb(f"bhlo{i}", [P, P], F32R) for i in range(2)]
        ones = sb("ones", [P, P])
        ident = sb("ident", [P, P])
        tri = sb("tri", [P, P])
        gatef = sb("gatef", [P, KC, E])
        gate = sb("gate", [P, KC, 2, E], F32R)
        wcol = sb("wcol", [P, KC])
        epst = sb("epst", [P, 1])
        agent = sb("agent", [P, B, TB])
        tok = sb("tok", [P, B, TB])
        tok2 = sb("tok2", [P, B, TB])
        lv = sb("lv", [P, B, TB])
        att = sb("att", [P, C])
        small = sb("small", [P, B, 8])
        bst = sb("bst", [P, G, 6])
        mv = sb("mv", [P, NT, 2])
        rstd = sb("rstd", [P, NT])
        rn = sb("rn", [P, 3, TB])
        fmv = sb("fmv", [P, G, 2])
        frn = sb("frn", [P, 4, G])
        top = sb("top", [P, NT, K])
        slot = sb("slot", [P, NT, K], I32)
        eid = sb("eid", [P, NT, K])
        place = sb("place", [P, NT, K], I32)
        rt = sb("rt", [P, 9, G, E])
        r4 = sb("r4", [P, 3, G])
        seen = sb("seen", [P, E])
        ebase = sb("ebase", [P, E])
        jota = sb("jota", [1, NBK])
        thr = sb("thr", [P, NT])
        te = sb("te", [1, 2, NBK])
        tc = sb("tc", [P, 6, E])
        clear = sb("clear", [P, C])
        m8 = sb("m8", [P, G, 8])
        i8 = sb("i8", [P, G, 8], mybir.dt.uint32)
        eota = sb("eota", [P, E])
        zrow = sb("zrow", [1, E], I32)
        brow = sb("brow", [1, NBK], I32)
        bexp = sb("bexp", [1, NBK], I32)
        banks = [ctx.enter_context(nc.psum_tensor(f"bank{n}", [P, 512], F32)) for n in range(8)]

        wq = mix[:, 0, :].rearrange("p (k c) -> p k c", k=KC)
        wv = mix[:, 1, :].rearrange("p (k c) -> p k c", k=KC)
        wkvt = mix[:, 2:4, :]
        sg = [mix[:, n, :] for n in range(2)]
        prod = [mix[:, 2 + n, :] for n in range(2)]
        wide = x2[0]
        junk = x2[1]
        flat = stage[:, 0, :]
        xg = [flat[:, n * C:(n + 1) * C] for n in range(2)]
        bsg = [flat[:, 512 + n * H:512 + (n + 1) * H] for n in range(2)]
        bprod = [flat[:, 896 + n * 2 * P:896 + (n + 1) * 2 * P] for n in range(2)]
        by = [flat[:, 1408 + n * C:1408 + (n + 1) * C] for n in range(2)]
        got = [[stage[:, k, n * G * C:(n + 1) * G * C].rearrange("p (t c) -> p t c", t=G) for n in range(2)]
               for k in range(K)]
        mvf = mv[:].rearrange("p t s -> p (t s)")
        topf = top[:].rearrange("p t k -> p (t k)")
        tokf = tok[:].rearrange("p b t -> p (b t)")
        agentf = agent[:].rearrange("p b t -> p (b t)")
        lvf = lv[:].rearrange("p b t -> p (b t)")

        bank_x, bank_y, bank_h, bank_t = banks[0:2], banks[2:4], banks[4:6], banks[6:8]

        s_x = [sem(f"x_loaded{b}") for b in range(B)]
        s_wq, s_wkv, s_gate = sem("wq_loaded"), sem("wkv_loaded"), sem("gate_loaded")
        s_raw = [sem(f"raw_loaded{n}") for n in range(5)]
        s_whi, s_wlo, s_gset = sem("weights_hi"), sem("weights_lo"), sem("gate_split")
        s_mem, s_set = sem("cleared"), sem("constants")
        s_pad = sem("padding_written")
        s_dve, s_pe, s_act, s_pool = sem("att_vector"), sem("att_tensor"), sem("att_scalar"), sem("att_pool")
        s_ag, s_lv, s_add, s_stat, s_agg = sem("agent"), sem("token_logits"), sem("att_added"), sem("ln1_sums"), sem("ln1_stats")

        s_x2, s_xtp, s_xhi, s_xt = sem("x2"), sem("x2t_psum"), sem("x2t_hi"), sem("x2t")
        s_lg, s_sh, s_ex, s_m = sem("logits"), sem("logits_shifted"), sem("exps"), sem("chosen")
        s_pos, s_slot, s_sc = sem("positions"), sem("slots"), pair("scattered")
        (s_lsum, s_lmax, s_esum, s_rcp, s_score, s_top8, s_idx, s_sel, s_place, s_tmp) = (
            sem(f"route_{n}") for n in ("logits", "max", "sum", "reciprocal", "scores", "top8", "index", "masks",
                                        "places", "terms"))
        s_h = [sem(f"hidden_psum{m}") for m in range(MC)]
        s_sg = [sem(f"silu{m}") for m in range(MC)]
        s_pr = [sem(f"product{m}") for m in range(MC)]
        s_hhi = [sem(f"hidden_hi{m}") for m in range(MC)]
        s_ht = sem("hidden")
        s_z = [sem(f"shared_psum{u}") for u in range(2)]
        s_zev = [sem(f"shared_added{u}") for u in range(2)]
        s_cnt, s_tb, s_tbl = sem("counts"), sem("table_steps"), sem("block_table")
        s_place_out = sem("result_places")

        s_ld, s_bxp, s_bxhi, s_bx = pair("rows_loaded"), pair("rows_t_psum"), pair("rows_t_hi"), pair("rows_t")
        s_bh, s_bsg, s_bpr = pair("expert_hidden"), pair("expert_silu"), pair("expert_product")
        s_bhp, s_bhhi, s_bht = pair("expert_ht_psum"), pair("expert_ht_hi"), pair("expert_ht")
        s_by, s_byev, s_st = pair("expert_out"), pair("expert_row"), pair("rows_stored")

        s_got, s_first, s_sum = pair("gathered"), sem("first_added"), sem("summed")
        s_bst, s_var, s_std = sem("ln2_sums"), sem("ln2_stats"), sem("ln2_std")
        s_n = [sem(f"ln2_newton{n}") for n in range(5)]
        s_fin, s_out, s_tick = sem("ln2_ready"), pair("out_stored"), sem("wait_taken")

        block = ctx.enter_context(nc.Block())

        DVE = ["tok_shift", "g", "max", "tok_rcp", "sum_rcp", "att", "tok", "col", "lmax", "lneg", "psum_rcp", "s",
               "std_rcp", "square", "times_var", "newton", "rstd"]
        PE = ["g", "logits", "col", "r", "s", "value"]
        SCALAR = ["tok_exp", "exp", "p", "std"]
        POOL = ["max", "sum"]

        def dve(b, name):
            return 2 + b * len(DVE) + DVE.index(name)

        def pe_at(b, name):
            return 2 + b * len(PE) + PE.index(name)

        def act_at(b, name):
            return 1 + b * len(SCALAR) + SCALAR.index(name)

        def pool_at(b, name):
            return 1 + b * len(POOL) + POOL.index(name)

        def sl(start, size=1):
            return slice(start, start + size) if isinstance(start, int) else bass.ds(start, size)

        def groups(eng, body):
            for n in (1, 2):
                body(n, (n - 1) % 2)
            with eng.Fori(2, NP + 1) as i:
                body(eng.snap(2 * i - 1), 0)
                body(eng.snap(2 * i), 1)

        def later(n, by=1):
            return not isinstance(n, int) or n > by

        def blocks(eng, step):
            def static(j):
                def at(d):
                    b = j + d
                    return (b // 2 + 1, b % 2) if 0 <= b < NBK else None
                return at
            for j in (-1, 0, 1):
                step(static(j))
            with eng.Fori(2, NBP) as i:
                before, after = eng.snap(i - 1), eng.snap(i + 1)
                near = {-2: (before, 0), -1: (before, 1), 0: (i, 0), 1: (i, 1), 2: (after, 0)}
                for par in range(2):
                    step(lambda d, par=par: near[par + d])
            for j in (NBK - 2, NBK - 1, NBK, NBK + 1):
                step(static(j))

        def block_id(c, par):
            return sl((c - 1) * 2 + par)

        S1 = KC * 2 * HS
        RAW = [stage[:, 0, 0:S1 + MC * C], stage[:, 1, 0:4 * KC * F], stage[:, 0, 0:4 * KC * F],
               stage[:, 1, 0:E * C], stage[:, 0, 0:E * C]]

        def parts(s1, s2, a, b, r):
            return [[(s1[:].rearrange("p k f -> p (k f)"), RAW[0][:, 0:S1]),
                     (s2[:].rearrange("p m c -> p (m c)"), RAW[0][:, S1:])],
                    [(a[:, 0:4].rearrange("p e k f -> p (e k f)"), RAW[1])],
                    [(a[:, 4:8].rearrange("p e k f -> p (e k f)"), RAW[2])],
                    [(b[:].rearrange("p e c -> p (e c)"), RAW[3])],
                    [(r[:].rearrange("p e c -> p (e c)"), RAW[4])]]

        HI = parts(ws1hi, ws2hi, w1hi, w2hi, w2rhi)
        LO = parts(ws1lo, ws2lo, w1lo, w2lo, w2rlo)
        SPLIT = [2, 3, 4, 5, 6]

        @block.sync
        def _(sp):
            sp.dma_start(xs[:, 0:TB, :], x[0].rearrange("(p j) c -> p j c", j=TB)).then_inc(s_x[0], 16)
            sp.dma_start(wq, w_qkv[0:C].rearrange("(k p) c -> p k c", p=P)).then_inc(s_wq, 16)
            sp.dma_start(wcol[:], w_conv).then_inc(s_wq, 16)
            sp.dma_start(wkvt, w_kv_t.rearrange("(k p) c -> p k c", p=P)).then_inc(s_wkv, 16)
            sp.dma_start(wv, w_qkv[2 * C:3 * C].rearrange("(k p) c -> p k c", p=P)).then_inc(s_wkv, 16)
            sp.dma_start(xs[:, TB:NT, :], x[1].rearrange("(p j) c -> p j c", j=TB)).then_inc(s_x[1], 16)
            sp.dma_start(gatef[:], gate_t.rearrange("(k p) e -> p k e", p=P)).then_inc(s_gate, 16)
            sp.dma_start(RAW[0][:, 0:S1].rearrange("p (k f) -> p k f", k=KC),
                         ws1_t.rearrange("(k p) f -> p k f", p=P)).then_inc(s_raw[0], 16)
            sp.dma_start(RAW[0][:, S1:].rearrange("p (m c) -> p m c", m=MC),
                         ws2_t.rearrange("(m p) c -> p m c", p=P)).then_inc(s_raw[0], 16)
            for n in range(2):
                if n == 1:
                    sp.wait_ge(s_whi, SPLIT[0])
                    sp.wait_ge(s_wlo, SPLIT[0])
                for e in range(4):
                    sp.dma_start(RAW[1 + n].rearrange("p (e k f) -> p e k f", e=4, k=KC)[:, e],
                                 w1_t[4 * n + e].rearrange("(k p) f -> p k f", p=P)).then_inc(s_raw[1 + n], 16)
            sp.wait_ge(s_whi, SPLIT[1])
            sp.wait_ge(s_wlo, SPLIT[1])
            sp.dma_start(RAW[3].rearrange("p (e c) -> p e c", e=E),
                         w2_t[:, 0:P].rearrange("e p c -> p e c")).then_inc(s_raw[3], 16)
            sp.wait_ge(s_whi, SPLIT[2])
            sp.wait_ge(s_wlo, SPLIT[2])
            for n in range(2):
                sp.dma_start(RAW[4][n * HR:(n + 1) * HR].rearrange("p (e c) -> p e c", e=E),
                             w2_t[:, P:H].rearrange("e p c -> p e c")).then_inc(s_raw[4], 16)
            sp.wait_ge(s_mem, 2)
            for n in range(IDLE):
                sp.dma_start(rows_in[E * CAP + n * P:E * CAP + (n + 1) * P, :], clear[:]).then_inc(s_pad, 16)
            sp.wait_ge(s_tbl, 1)
            for e in range(E):
                r = sp.value_load(zrow[0:1, e:e + 1], min_val=0, max_val=ROWS - P)
                sp.dma_start(rows_in[bass.ds(r, P), :], clear[:]).then_inc(s_pad, 16)
            for n in range(2):
                sp.wait_ge(s_sc[n], 16 * K * G * NP)
            sp.wait_ge(s_pad, 16 * (IDLE + E))
            sp.wait_ge(s_whi, SPLIT[4])
            sp.wait_ge(s_wlo, SPLIT[4])

            def step(at):
                if load := at(1):
                    c, par = load
                    if not (isinstance(c, int) and c == 1):
                        sp.wait_ge(s_bxp[par], c - 1)
                    r = sp.value_load(brow[0:1, block_id(c, par)], min_val=0, max_val=ROWS - P)
                    sp.dma_start(xg[par], rows_in[bass.ds(r, P), :]).then_inc(s_ld[par], 16)
                if store := at(-2):
                    c, par = store
                    sp.wait_ge(s_byev[par], c)
                    sp.dma_start(rows_out[sl(((c - 1) * 2 + par) * P, P), :], by[par]).then_inc(s_st[par], 16)

            blocks(sp, step)
            for q in range(NG):
                sp.wait_ge(s_fin, q + 1)
                n = q * G
                sp.dma_start(out[n // TB].rearrange("(p j) c -> p j c", j=TB)[:, n % TB:n % TB + G, :],
                             got[0][q % 2]).then_inc(s_out[q % 2], 16)
            for par in range(2):
                sp.wait_ge(s_out[par], 16 * NP)

        @block.gpsimd
        def _(pool):
            pool.memset(ones[:], 1.0).then_inc(s_mem, 1)
            pool.memset(ident[:], 0.0)
            pool.memset(epst[:], EPS)
            pool.memset(seen[:], 0.0)
            pool.memset(tri[:], 1.0)
            pool.memset(clear[:], 0.0).then_inc(s_mem, 1)
            pool.wait_ge(s_mem, 2)
            pool.affine_select(out=ident[:], in_=ident[:], compare_op=ALU.not_equal, fill=1.0, base=0,
                               pattern=[[-1, P]], channel_multiplier=1)
            pool.affine_select(out=tri[:], in_=tri[:], compare_op=ALU.is_gt, fill=0.0, base=0,
                               pattern=[[1, P]], channel_multiplier=-1)
            pool.iota(ebase[:], [[CAP, E]], base=0, channel_multiplier=0, allow_small_or_imprecise_dtypes=True)
            pool.iota(eota[:], [[1, E]], base=0, channel_multiplier=0, allow_small_or_imprecise_dtypes=True)
            pool.iota(jota[:], [[1, NBK]], base=0, channel_multiplier=0, allow_small_or_imprecise_dtypes=True)
            pool.iota(thr[:], [[P, NT]], base=0, channel_multiplier=0,
                      allow_small_or_imprecise_dtypes=True).then_inc(s_set, 1)

            def low(n):
                for m, (dst, src) in enumerate(LO[n]):
                    pool.wait_ge(s_whi, SPLIT[n])
                    pool.tensor_tensor(dst, src, HI[n][m][0].bitcast(F32), ALU.subtract).then_inc(s_wlo, 1)

            low(0)
            for b in range(B):
                pool.wait_ge(s_dve, dve(b, "lmax"))
                pool.partition_all_reduce(small[:, b, 3:4], small[:, b, 2:3], P, RMAX).then_inc(s_pool, 1)
                pool.wait_ge(s_act, act_at(b, "p"))
                pool.partition_all_reduce(small[:, b, 6:7], small[:, b, 5:6], P, RADD).then_inc(s_pool, 1)
            for n in range(1, 5):
                low(n)
            for q in range(NG):
                pool.wait_ge(s_slot, q + 1)
                for t in range(G):
                    for k in range(K):
                        pool.indirect_dma_start(
                            rows_in[0:E * CAP, :], bass.IndirectOffsetOnAxis(slot[:, q * G + t, k:k + 1], 0),
                            x2[q % 2][:, t, :], None).then_inc(s_sc[q % 2], 16)
            for n in range(2):
                pool.wait_ge(s_st[n], 16 * NBP)
            pool.wait_ge(s_place_out, 1)
            for q in range(NG):
                if q >= 2:
                    pool.wait_ge(s_out[q % 2], 16 * (q // 2))
                for t in range(G):
                    for k in range(K):
                        pool.indirect_dma_start(
                            got[k][q % 2][:, t, :], None, rows_out[:, :],
                            bass.IndirectOffsetOnAxis(place[:, q * G + t, k:k + 1], 0)).then_inc(s_got[q % 2], 16)

        @block.scalar
        def _(act):
            def high(n, dmas):
                act.wait_ge(s_raw[n], 16 * dmas)
                for dst, src in HI[n]:
                    act.activation(dst, src, ACT.Copy).then_inc(s_whi, 1)

            high(0, 2)
            for b in range(B):
                act.wait_ge(s_dve, dve(b, "tok_shift"))
                act.activation(tok[:, b, :], tok2[:, b, :], ACT.Exp).then_inc(s_act, 1)
                act.wait_ge(s_dve, dve(b, "max"))
                act.activation(att[:], banks[2][:, b * C:(b + 1) * C], ACT.Exp, bias=small[:, b, 0:1],
                               accum_out=small[:, b, 1:2]).then_inc(s_act, 1)
                act.wait_ge(s_dve, dve(b, "lneg"))
                act.activation(lv[:, b, :], lv[:, b, :], ACT.Exp, bias=small[:, b, 4:5],
                               accum_out=small[:, b, 5:6]).then_inc(s_act, 1)
                high(1 + b, 4)
                act.wait_ge(s_agg, NP * (b + 1))
                act.activation(rn[:, 0, :], mv[:, b * TB:(b + 1) * TB, 1], ACT.Sqrt, bias=epst[:]).then_inc(s_act, 1)
            high(3, 1)
            high(4, 2)

            def group(n, par):
                act.wait_ge(s_xtp, n)
                if later(n):
                    act.wait_ge(s_h[MC - 1], n - 1)
                for k in range(KC):
                    ins = act.activation(xthi[:, k, :], banks[k][:], ACT.Copy)
                ins.then_inc(s_xhi, 1)
                act.wait_ge(s_sh, n)
                act.activation(rt[:, 2], rt[:, 1], ACT.Exp).then_inc(s_ex, 1)

                def silu(m):
                    buf = (par + m) % 2
                    act.wait_ge(s_h[m], n)
                    act.activation(sg[buf], banks[5 + 2 * buf][:], ACT.Silu).then_inc(s_sg[m], 1)

                def hidden(m):
                    act.wait_ge(s_pr[m], n)
                    act.activation(hthi[:, m, :], prod[(par + m) % 2], ACT.Copy).then_inc(s_hhi[m], 1)

                silu(0)
                silu(1)
                if later(n):
                    act.wait_ge(s_z[1], n - 1)
                hidden(0)
                silu(2)
                hidden(1)
                hidden(2)

            groups(act, group)
            act.preload_act_table(ACT.Silu)

            def step(at):
                if rows := at(1):
                    c, par = rows
                    act.wait_ge(s_bxp[par], c)
                    act.activation(bxhi[par][:].rearrange("p k t -> p (k t)"), bank_x[par][:, 0:C],
                                   ACT.Copy).then_inc(s_bxhi[par], 1)
                if now := at(0):
                    c, par = now
                    act.wait_ge(s_bh[par], c)
                    act.activation(bsg[par], bank_h[par][:, H:F], ACT.Silu).then_inc(s_bsg[par], 1)
                if hidden := at(-1):
                    c, par = hidden
                    act.wait_ge(s_bhp[par], c)
                    act.activation(bhhi[par][:].rearrange("p k t -> p (k t)"), bank_t[par][:, 0:2 * P],
                                   ACT.Copy).then_inc(s_bhhi[par], 1)
                if result := at(-2):
                    c, par = result
                    act.wait_ge(s_by[par], c)
                    if not (isinstance(c, int) and c == 1):
                        act.wait_ge(s_st[par], 16 * (c - 1))
                    act.activation(by[par], bank_y[par][:, 0:C], ACT.Copy).then_inc(s_byev[par], 1)

            blocks(act, step)
            act.preload_act_table(ACT.Sqrt)
            with act.Fori(1, NG + 1) as n:
                act.wait_ge(s_var, n)
                act.activation(frn[:, 0, :], fmv[:, :, 1], ACT.Sqrt, bias=epst[:]).then_inc(s_std, 1)

        @block.tensor
        def _(pe):
            pe.wait_ge(s_wq, 32)
            pe.wait_ge(s_dve, 1)
            for k in range(KC):
                mm = pe.matmul(banks[0][:, 0:C], wide[:, 0, k * P:(k + 1) * P], wq[:, k, :],
                               start=(k == 0), stop=(k == KC - 1))
            mm.then_inc(s_pe, 1)

            def weighted_sum(bank, b, weight):
                for k in range(KC):
                    for t in range(TB):
                        mm = pe.matmul(bank[:, 8 * b + k:8 * b + k + 1], xs[:, b * TB + t, k * P:(k + 1) * P],
                                       weight[:, b, t:t + 1], start=(t == 0), stop=(t == TB - 1))
                return mm

            def with_matrix(bank, b, spread, matrix):
                for k in range(KC):
                    mm = pe.matmul(bank[:, b * C:(b + 1) * C], spread[:, 1 + b, k * P:(k + 1) * P], matrix(k),
                                   start=(k == 0), stop=(k == KC - 1))
                return mm

            for b in range(B):
                pe.wait_ge(s_ag, TB * (b + 1))
                weighted_sum(banks[1], b, agent).then_inc(s_pe, 1)
                pe.wait_ge(s_dve, dve(b, "g"))
                pe.wait_ge(s_wkv, 32)
                with_matrix(banks[2], b, wide, lambda k: wkvt[:, k, 0:C]).then_inc(s_pe, 1)
                pe.wait_ge(s_dve, dve(b, "att"))
                for k in range(KC):
                    mm = pe.matmul(banks[3][:, 8 * b + k:8 * b + k + 1], att[0:1, k * P:(k + 1) * P], ones[0:1, 0:1],
                                   start=True, stop=True)
                mm.then_inc(s_pe, 1)
                pe.wait_ge(s_dve, dve(b, "col"))
                with_matrix(banks[4], b, wide, lambda k: wv[:, k, :]).then_inc(s_pe, 1)
                pe.wait_ge(s_act, act_at(b, "p"))
                weighted_sum(banks[5], b, lv).then_inc(s_pe, 1)
                pe.wait_ge(s_dve, dve(b, "s"))
                with_matrix(banks[6], b, wide, lambda k: wkvt[:, k, C:2 * C]).then_inc(s_pe, 1)

            pe.wait_ge(s_set, 1)
            pe.wait_ge(s_gset, 2)
            pe.wait_ge(s_wlo, SPLIT[0])

            def group(n, par):
                pe.wait_ge(s_x2, n)
                if later(n):
                    pe.wait_ge(s_zev[0], n - 1)
                for k in range(KC):
                    for t in range(G):
                        mm = pe.transpose(banks[k][:, t * P:(t + 1) * P], x2[par][:, t, k * P:(k + 1) * P], ident[:])
                mm.then_inc(s_xtp, 1)
                pe.wait_ge(s_xt, n)
                for t in range(G):
                    steps = [(xt, k) for xt in (xthi, xtlo) for k in range(KC)]
                    for a, (xt, k) in enumerate(steps):
                        mm = pe.matmul(banks[2][:, t * 2 * E:(t + 1) * 2 * E], xt[:, k, t * P:(t + 1) * P],
                                       gate[:, k].rearrange("p h e -> p (h e)"),
                                       start=(a == 0), stop=(a == len(steps) - 1))
                mm.then_inc(s_lg, 1)
                for m in range(MC):
                    buf = (par + m) % 2
                    if m == 2:
                        pe.wait_ge(s_pr[0], n)
                    elif later(n):
                        pe.wait_ge(s_pr[m + 1], n - 1)
                    for o, bank in ((m * P, banks[4 + 2 * buf]), (HS + m * P, banks[5 + 2 * buf])):
                        steps = [(w, xt, k) for w, xt in ((ws1hi, xthi), (ws1hi, xtlo), (ws1lo, xthi)) for k in range(KC)]
                        for a, (w, xt, k) in enumerate(steps):
                            mm = pe.matmul(bank[:], w[:, k, o:o + P], xt[:, k, :],
                                           start=(a == 0), stop=(a == len(steps) - 1))
                    mm.then_inc(s_h[m], 1)
                pe.wait_ge(s_m, n)
                chosen = rt[:, 7].rearrange("p t e -> p (t e)")
                pe.matmul(banks[2][:, 64:64 + G * E], tri[:], chosen, start=True, stop=False)
                for d in range(1, G):
                    pe.matmul(banks[2][:, 64 + d * E:64 + G * E], ones[:], chosen[:, 0:(G - d) * E],
                              start=False, stop=False)
                pe.matmul(banks[2][:, 64:64 + G * E].rearrange("p (t e) -> p t e", t=G), ones[:],
                          seen[:].unsqueeze(1).broadcast_to([P, G, E]), start=False, stop=True).then_inc(s_pos, 1)
                pe.wait_ge(s_ht, n)
                for u, bank in enumerate((banks[1], banks[3])):
                    if u == 1 and later(n):
                        pe.wait_ge(s_zev[1], n - 1)
                    for t in (2 * u, 2 * u + 1):
                        steps = [(ht, w, m) for ht, w in ((hthi, ws2hi), (htlo, ws2hi), (hthi, ws2lo)) for m in range(MC)]
                        for a, (ht, w, m) in enumerate(steps):
                            mm = pe.matmul(bank[:, (t % 2) * C:(t % 2 + 1) * C], ht[:, m, t * P:(t + 1) * P], w[:, m, :],
                                           start=(a == 0), stop=(a == len(steps) - 1))
                    mm.then_inc(s_z[u], 1)

            groups(pe, group)
            pe.wait_ge(s_slot, NG)
            pe.matmul(banks[2][:, 128:128 + E], ones[:], seen[:], start=True, stop=True).then_inc(s_cnt, 1)
            pe.wait_ge(s_tbl, 1)
            pe.wait_ge(s_wlo, SPLIT[4])

            def step(at):
                if rows := at(1):
                    c, par = rows
                    pe.wait_ge(s_ld[par], 16 * c)
                    for k in range(KC):
                        mm = pe.transpose(bank_x[par][:, k * P:(k + 1) * P], xg[par][:, k * P:(k + 1) * P], ident[:])
                    mm.then_inc(s_bxp[par], 1)
                if now := at(0):
                    c, par = now
                    e = pe.value_load(bexp[0:1, block_id(c, par)], min_val=0, max_val=E - 1)
                    pe.wait_ge(s_bx[par], c)
                    steps = [(bx, w, k) for bx, w in ((bxhi, w1hi), (bxlo, w1hi), (bxhi, w1lo)) for k in range(KC)]
                    for a, (bx, w, k) in enumerate(steps):
                        mm = pe.matmul(bank_h[par][:, 0:F], bx[par][:, k, :], w[:, bass.ds(e, 1), k, :],
                                       start=(a == 0), stop=(a == len(steps) - 1))
                    mm.then_inc(s_bh[par], 1)
                if hidden := at(-1):
                    c, par = hidden
                    pe.wait_ge(s_bpr[par], c)
                    for k in range(2):
                        mm = pe.transpose(bank_t[par][:, k * P:(k + 1) * P], bprod[par][:, k * P:(k + 1) * P], ident[:])
                    mm.then_inc(s_bhp[par], 1)
                if result := at(-2):
                    c, par = result
                    e = pe.value_load(bexp[0:1, block_id(c, par)], min_val=0, max_val=E - 1)
                    pe.wait_ge(s_bht[par], c)
                    if not (isinstance(c, int) and c == 1):
                        pe.wait_ge(s_byev[par], c - 1)
                    first, second = bhhi[par][:, 0, :], bhhi[par][:, 1, :]
                    steps = [(first, w2hi), (bhlo[par][:], w2hi), (first, w2lo), (second, w2rhi), (second, w2rlo)]
                    for a, (ht, w) in enumerate(steps):
                        mm = pe.matmul(bank_y[par][:, 0:C], ht, w[:, bass.ds(e, 1), :],
                                       start=(a == 0), stop=(a == len(steps) - 1))
                    mm.then_inc(s_by[par], 1)

            blocks(pe, step)

        @block.vector
        def _(vec):
            def spread(dst, col, b, scale):
                for k in range(KC):
                    ins = vec.tensor_scalar(dst[:, k * P:(k + 1) * P], ones[:], col[:, k:k + 1], scale, ALU.mult, ALU.mult)
                return ins

            vec.wait_ge(s_wq, 32)
            vec.wait_ge(s_mem, 1)
            spread(wide[:, 0, :], wcol, 0, 1.0).then_inc(s_dve, 1)
            vec.wait_ge(s_gate, 16)
            vec.tensor_copy(gate[:, :, 0, :], gatef[:]).then_inc(s_gset, 1)
            vec.wait_ge(s_gset, 1)
            vec.tensor_tensor(gate[:, :, 1, :], gatef[:], gate[:, :, 0, :].bitcast(F32), ALU.subtract).then_inc(s_gset, 1)

            def dots(row, dst, b, done):
                for t in range(b * TB, (b + 1) * TB):
                    if t >= G:
                        vec.wait_ge(done, t - G + 1)
                    vec.tensor_tensor_reduce(junk[:, t % G, :], xs[:, t, :], row, 1.0, 0.0, ALU.mult, ALU.add,
                                             dst[:, t:t + 1]).then_inc(done, 1)

            vec.wait_ge(s_pe, 1)
            for b in range(B):
                vec.wait_ge(s_x[b], 16)
                dots(banks[0][:, 0:C], agentf, b, s_ag)

            for b in range(B):
                c8 = slice(8 * b, 8 * b + KC)
                vec.wait_ge(s_ag, TB * (b + 1))
                vec.tensor_tensor(tok2[:, b, :], agent[:, b, :], agent[:, b, :], ALU.subtract).then_inc(s_dve, 1)
                vec.wait_ge(s_pe, pe_at(b, "g"))
                spread(wide[:, 1 + b, :], banks[1][:, c8], b, SCALE).then_inc(s_dve, 1)
                vec.wait_ge(s_pe, pe_at(b, "logits"))
                vec.tensor_reduce(small[:, b, 0:1], banks[2][:, b * C:(b + 1) * C], AX.X, ALU.max,
                                  negate=True).then_inc(s_dve, 1)
                vec.wait_ge(s_act, act_at(b, "tok_exp"))
                vec.reciprocal(tok2[:, b, :], tok[:, b, :]).then_inc(s_dve, 1)
                vec.wait_ge(s_act, act_at(b, "exp"))
                vec.reciprocal(small[:, b, 7:8], small[:, b, 1:2]).then_inc(s_dve, 1)
                vec.wait_ge(s_dve, dve(b, "sum_rcp"))
                vec.tensor_scalar(att[0:1, :], att[0:1, :], small[0:1, b, 7:8], None, ALU.mult).then_inc(s_dve, 1)
                vec.tensor_tensor(tok[:, b, :], tok[:, b, :], tok2[:, b, :], ALU.mult).then_inc(s_dve, 1)
                vec.wait_ge(s_pe, pe_at(b, "col"))
                spread(wide[:, 1 + b, :], banks[3][:, c8], b, 1.0).then_inc(s_dve, 1)
                vec.wait_ge(s_pe, pe_at(b, "r"))
                dots(banks[4][:, b * C:(b + 1) * C], lvf, b, s_lv)
                vec.wait_ge(s_lv, TB * (b + 1))
                vec.tensor_reduce(small[:, b, 2:3], lv[:, b, :], AX.X, ALU.max).then_inc(s_dve, 1)
                vec.wait_ge(s_pool, pool_at(b, "max"))
                vec.tensor_scalar(small[:, b, 4:5], small[:, b, 3:4], -1.0, None, ALU.mult).then_inc(s_dve, 1)
                vec.wait_ge(s_pool, pool_at(b, "sum"))
                vec.reciprocal(small[:, b, 7:8], small[:, b, 6:7]).then_inc(s_dve, 1)
                vec.wait_ge(s_pe, pe_at(b, "s"))
                vec.wait_ge(s_dve, dve(b, "psum_rcp"))
                spread(wide[:, 1 + b, :], banks[5][:, c8], b, small[:, b, 7:8]).then_inc(s_dve, 1)
                vec.wait_ge(s_pe, pe_at(b, "value"))
                for g in range(b * NP, (b + 1) * NP):
                    for t in range(g * G, (g + 1) * G):
                        ins = vec.scalar_tensor_tensor(xs[:, t, :], banks[6][:, b * C:(b + 1) * C], tokf[:, t:t + 1],
                                                       xs[:, t, :], ALU.mult, ALU.add)
                    ins.then_inc(s_add, 1)
                    vec.wait_ge(s_add, g + 1)
                    for t in range(G):
                        ins = vec.bn_stats(bst[:, t, :], xs[:, g * G + t, :])
                    ins.then_inc(s_stat, 1)
                    vec.wait_ge(s_stat, g + 1)
                    for t in range(G):
                        ins = vec.bn_aggr(mv[:, g * G + t, :], bst[:, t, :])
                    ins.then_inc(s_agg, 1)
                var = mv[:, b * TB:(b + 1) * TB, 1]
                vec.wait_ge(s_act, act_at(b, "std"))
                vec.reciprocal(rn[:, 1, :], rn[:, 0, :]).then_inc(s_dve, 1)
                vec.wait_ge(s_dve, dve(b, "std_rcp"))
                vec.tensor_tensor(rn[:, 2, :], rn[:, 1, :], rn[:, 1, :], ALU.mult).then_inc(s_dve, 1)
                vec.wait_ge(s_dve, dve(b, "square"))
                vec.scalar_tensor_tensor(rn[:, 2, :], var, EPS, rn[:, 2, :], ALU.add, ALU.mult).then_inc(s_dve, 1)
                vec.wait_ge(s_dve, dve(b, "times_var"))
                vec.tensor_scalar(rn[:, 2, :], rn[:, 2, :], -0.5, 1.5, ALU.mult, ALU.add).then_inc(s_dve, 1)
                vec.wait_ge(s_dve, dve(b, "newton"))
                vec.tensor_tensor(rstd[:, b * TB:(b + 1) * TB], rn[:, 1, :], rn[:, 2, :], ALU.mult).then_inc(s_dve, 1)

            vec.wait_ge(s_dve, dve(B - 1, "rstd"))
            vec.wait_ge(s_set, 1)

            def group(n, par):
                tile = (n - 1) * G if isinstance(n, int) else vec.snap((n - 1) * G)
                if later(n, 2):
                    vec.wait_ge(s_sc[par], (n - 1 - par) * (16 * K * G // 2))
                for t in range(G):
                    ins = vec.tensor_scalar(x2[par][:, t:t + 1, :], xs[:, sl(tile + t), :], mvf[:, sl(2 * (tile + t))],
                                            rstd[:, sl(tile + t)], ALU.subtract, ALU.mult)
                ins.then_inc(s_x2, 1)
                vec.wait_ge(s_xhi, n)
                for k in range(KC):
                    ins = vec.tensor_tensor(xtlo[:, k, :], banks[k][:], xthi[:, k, :].bitcast(F32), ALU.subtract)
                ins.then_inc(s_xt, 1)
                vec.wait_ge(s_lg, n)
                vec.tensor_reduce(rt[:, 0], banks[2][:, 0:2 * G * E].rearrange("p (t h e) -> p t e h", t=G, h=2), AX.X,
                                  ALU.add).then_inc(s_lsum, 1)
                vec.wait_ge(s_lsum, n)
                vec.tensor_reduce(r4[:, 0], rt[:, 0], AX.X, ALU.max).then_inc(s_lmax, 1)
                vec.wait_ge(s_lmax, n)
                vec.tensor_tensor(rt[:, 1], rt[:, 0], r4[:, 0].unsqueeze(2).broadcast_to([P, G, E]),
                                  ALU.subtract).then_inc(s_sh, 1)
                vec.wait_ge(s_ex, n)
                vec.tensor_reduce(r4[:, 1], rt[:, 2], AX.X, ALU.add).then_inc(s_esum, 1)
                vec.wait_ge(s_esum, n)
                vec.reciprocal(r4[:, 2], r4[:, 1]).then_inc(s_rcp, 1)
                vec.wait_ge(s_rcp, n)
                vec.tensor_tensor(rt[:, 3], rt[:, 2], r4[:, 2].unsqueeze(2).broadcast_to([P, G, E]),
                                  ALU.mult).then_inc(s_score, 1)
                vec.wait_ge(s_score, n)
                vec.sem_inc(s_tick, 1)
                for t in range(G):
                    ins = vec.max(m8[:, t, :], rt[:, 3, t, :])
                ins.then_inc(s_top8, 1)
                vec.wait_ge(s_top8, n)
                vec.sem_inc(s_tick, 1)
                for t in range(G):
                    ins = vec.max_index(i8[:, t, :], m8[:, t, :], rt[:, 3, t, :])
                ins.then_inc(s_idx, 1)
                vec.tensor_copy(top[:, sl(tile, G), :], m8[:, :, 0:K])
                vec.wait_ge(s_idx, n)
                for k in range(K):
                    ins = vec.tensor_tensor(rt[:, 5 + k], eota[:].unsqueeze(1).broadcast_to([P, G, E]),
                                            i8[:, :, k:k + 1].broadcast_to([P, G, E]), ALU.is_equal)
                ins.then_inc(s_sel, 1)
                vec.tensor_copy(eid[:, sl(tile, G), :], i8[:, :, 0:K])
                vec.wait_ge(s_sel, n)
                vec.tensor_tensor(rt[:, 7], rt[:, 5], rt[:, 6], ALU.add).then_inc(s_m, 1)
                for m in range(MC):
                    buf = (par + m) % 2
                    vec.wait_ge(s_sg[m], n)
                    vec.tensor_tensor(prod[buf], banks[4 + 2 * buf][:], sg[buf], ALU.mult).then_inc(s_pr[m], 1)
                    vec.wait_ge(s_hhi[m], n)
                    ins = vec.tensor_tensor(htlo[:, m, :], prod[buf], hthi[:, m, :].bitcast(F32), ALU.subtract)
                ins.then_inc(s_ht, 1)
                vec.wait_ge(s_pos, n)
                vec.tensor_tensor(rt[:, 8], banks[2][:, 64:64 + G * E].rearrange("p (t e) -> p t e", t=G),
                                  ebase[:].unsqueeze(1).broadcast_to([P, G, E]), ALU.add).then_inc(s_place, 1)
                vec.tensor_reduce(rt[:, 4, 0, :], rt[:, 7].rearrange("p t e -> p e t"), AX.X, ALU.add)
                vec.wait_ge(s_place, n)
                for k in range(K):
                    ins = vec.tensor_tensor(rt[:, 5 + k], rt[:, 5 + k], rt[:, 8], ALU.mult)
                ins.then_inc(s_tmp, 1)
                vec.wait_ge(s_tmp, n)
                vec.tensor_tensor(seen[:], seen[:], rt[:, 4, 0, :], ALU.add)
                for k in range(K):
                    with nc.allow_low_precision(reason="row numbers below 2**24: exact"):
                        ins = vec.tensor_reduce(slot[:, sl(tile, G), k:k + 1], rt[:, 5 + k], AX.X, ALU.add)
                ins.then_inc(s_slot, 1)
                for u, bank in enumerate((banks[1], banks[3])):
                    vec.wait_ge(s_z[u], n)
                    vec.tensor_tensor(xs[:, sl(tile + 2 * u, 2), :], bank[:].rearrange("p (t c) -> p t c", t=2),
                                      x2[par][:, 2 * u:2 * u + 2, :], ALU.add).then_inc(s_zev[u], 1)

            groups(vec, group)

            steps = [0]

            def table(ins):
                steps[0] += 1
                ins.then_inc(s_tb, 1)
                vec.wait_ge(s_tb, steps[0])

            count, nblk, last, unit, shift = (tc[:, n, :] for n in range(5))
            bid, start = te[:, 0, :], te[:, 1, :]
            space = stage[:, 1, :]
            grid = [space[0:1, n * NBK * E:(n + 1) * NBK * E].rearrange("p (j e) -> p j e", e=E) for n in range(2)]
            over = space[:, 2 * NBK * E:2 * NBK * E + E * NT].rearrange("p (e t) -> p e t", e=E)
            own = [space[:, 1408 + n * NT * K * E:1408 + (n + 1) * NT * K * E].rearrange("p (s e) -> p s e", e=E)
                   for n in range(2)]
            flat_k = [a[:].rearrange("p t k -> p (t k)") for a in (eid, slot, place)]
            vec.wait_ge(s_cnt, 1)
            vec.wait_ge(s_wlo, SPLIT[4])
            vec.memset(unit, 1.0)
            table(vec.tensor_copy(count, banks[2][:, 128:128 + E]))
            vec.tensor_tensor(zrow[:], count[0:1, :], ebase[0:1, :], ALU.add)
            table(vec.tensor_tensor(over, thr[:].unsqueeze(1).broadcast_to([P, E, NT]),
                                    count.unsqueeze(2).broadcast_to([P, E, NT]), ALU.is_lt))
            table(vec.tensor_reduce(nblk, over, AX.X, ALU.add))
            table(vec.tensor_tensor_scan(last, unit, nblk, 0.0, ALU.mult, ALU.add))
            table(vec.tensor_tensor(grid[0], jota[:].unsqueeze(2).broadcast_to([1, NBK, E]),
                                    last[0:1, :].unsqueeze(1).broadcast_to([1, NBK, E]), ALU.is_ge))
            table(vec.tensor_tensor(grid[1], grid[0], nblk[0:1, :].unsqueeze(1).broadcast_to([1, NBK, E]), ALU.mult))
            vec.tensor_reduce(bid, grid[0], AX.X, ALU.add)
            table(vec.tensor_reduce(start, grid[1], AX.X, ALU.add))
            vec.tensor_scalar(bexp[:], bid, float(E - 1), None, ALU.min)
            table(vec.tensor_tensor(start, jota[:], start, ALU.subtract))
            table(vec.tensor_scalar(bid, bid, float(CAP), None, ALU.mult))
            table(vec.scalar_tensor_tensor(brow[:], start, float(P), bid, ALU.mult, ALU.add))
            vec.engine_nop().then_inc(s_tbl, 1)
            table(vec.tensor_tensor(shift, last, nblk, ALU.subtract))
            table(vec.scalar_tensor_tensor(shift, shift, float(P), ebase[:], ALU.mult, ALU.subtract))
            table(vec.tensor_tensor(own[0], eota[:].unsqueeze(1).broadcast_to([P, NT * K, E]),
                                    flat_k[0].unsqueeze(2).broadcast_to([P, NT * K, E]), ALU.is_equal))
            table(vec.tensor_tensor(own[1], own[0], shift.unsqueeze(1).broadcast_to([P, NT * K, E]), ALU.mult))
            table(vec.tensor_reduce(flat_k[0], own[1], AX.X, ALU.add))
            vec.tensor_tensor(flat_k[2], flat_k[1], flat_k[0], ALU.add).then_inc(s_place_out, 1)

            def step(at):
                if rows := at(1):
                    c, par = rows
                    vec.wait_ge(s_bxhi[par], c)
                    vec.tensor_tensor(bxlo[par][:].rearrange("p k t -> p (k t)"), bank_x[par][:, 0:C],
                                      bxhi[par][:].rearrange("p k t -> p (k t)").bitcast(F32),
                                      ALU.subtract).then_inc(s_bx[par], 1)
                if now := at(0):
                    c, par = now
                    vec.wait_ge(s_bsg[par], c)
                    vec.tensor_tensor(bprod[par][:, 0:H], bank_h[par][:, 0:H], bsg[par], ALU.mult)
                    vec.tensor_tensor(bprod[par][:, H:2 * P], bank_h[par][:, P:H], bsg[par][:, P:H],
                                      ALU.mult).then_inc(s_bpr[par], 1)
                if hidden := at(-1):
                    c, par = hidden
                    vec.wait_ge(s_bhhi[par], c)
                    vec.tensor_tensor(bhlo[par][:], bank_t[par][:, 0:P], bhhi[par][:, 0, :].bitcast(F32), ALU.subtract)
                    vec.tensor_tensor(bhhi[par][HR:P, 1, :], bank_t[par][HR:P, P:2 * P],
                                      bhhi[par][HR:P, 1, :].bitcast(F32), ALU.subtract).then_inc(s_bht[par], 1)

            blocks(vec, step)

            def final(n, par):
                tile = (n - 1) * G if isinstance(n, int) else vec.snap((n - 1) * G)
                vec.wait_ge(s_got[par], (n + 1 - par) * (16 * K * G // 2))
                z = got[0][par]
                for t in range(G):
                    ins = vec.scalar_tensor_tensor(z[:, t:t + 1, :], z[:, t:t + 1, :], topf[:, sl((tile + t) * K)],
                                                   xs[:, sl(tile + t), :], ALU.mult, ALU.add)
                ins.then_inc(s_first, 1)
                vec.wait_ge(s_first, n)
                for t in range(G):
                    ins = vec.scalar_tensor_tensor(z[:, t:t + 1, :], got[1][par][:, t:t + 1, :],
                                                   topf[:, sl((tile + t) * K + 1)], z[:, t:t + 1, :], ALU.mult, ALU.add)
                ins.then_inc(s_sum, 1)
                vec.wait_ge(s_sum, n)
                for t in range(G):
                    ins = vec.bn_stats(bst[:, t, :], z[:, t, :])
                ins.then_inc(s_bst, 1)
                vec.wait_ge(s_bst, n)
                vec.sem_inc(s_tick, 1)
                for t in range(G):
                    ins = vec.bn_aggr(fmv[:, t, :], bst[:, t, :])
                ins.then_inc(s_var, 1)
                vec.wait_ge(s_std, n)
                vec.reciprocal(frn[:, 1, :], frn[:, 0, :]).then_inc(s_n[0], 1)
                vec.wait_ge(s_n[0], n)
                vec.tensor_tensor(frn[:, 2, :], frn[:, 1, :], frn[:, 1, :], ALU.mult).then_inc(s_n[1], 1)
                vec.wait_ge(s_n[1], n)
                vec.scalar_tensor_tensor(frn[:, 2, :], fmv[:, :, 1], EPS, frn[:, 2, :], ALU.add, ALU.mult).then_inc(s_n[2], 1)
                vec.wait_ge(s_n[2], n)
                vec.tensor_scalar(frn[:, 2, :], frn[:, 2, :], -0.5, 1.5, ALU.mult, ALU.add).then_inc(s_n[3], 1)
                vec.wait_ge(s_n[3], n)
                vec.tensor_tensor(frn[:, 3, :], frn[:, 1, :], frn[:, 2, :], ALU.mult).then_inc(s_n[4], 1)
                vec.wait_ge(s_n[4], n)
                for t in range(G):
                    ins = vec.tensor_scalar(z[:, t, :], z[:, t, :], fmv[:, t, 0:1], frn[:, 3, t:t + 1], ALU.subtract,
                                            ALU.mult)
                ins.then_inc(s_fin, 1)

            groups(vec, final)


def kernel(**inputs):
    import concourse.bacc as bacc
    from concourse.bass_utils import run_bass_kernel_spmd

    def laid(a, *axes):
        return np.ascontiguousarray(np.transpose(inputs[a], axes) if axes else inputs[a])

    nc = bacc.Bacc("TRN2", target_bir_lowering=False, num_devices=1)
    arrays = {
        "x": laid("L0_attn_x"),
        "w_qkv": laid("L0_attn_w_qkv"),
        "w_kv_t": np.ascontiguousarray(np.transpose(inputs["L0_attn_w_qkv"])[:, C:]),
        "w_conv": np.ascontiguousarray(np.reshape(inputs["L0_attn_w_conv1"], (KC, P)).T),
        "gate_t": laid("L0_ffn_gate_w", 1, 0),
        "w1_t": laid("L0_ffn_W1", 0, 2, 1),
        "w2_t": laid("L0_ffn_W2", 0, 2, 1),
        "ws1_t": laid("L0_ffn_Ws1", 1, 0),
        "ws2_t": laid("L0_ffn_Ws2", 1, 0),
    }
    args = [nc.dram_tensor(n, a.shape, mybir.dt.from_np(a.dtype), kind="ExternalInput").ap() for n, a in arrays.items()]
    out = nc.dram_tensor("out", (B, N, C), F32, kind="ExternalOutput").ap()
    post_norm_layer(nc, *args, out)
    r = run_bass_kernel_spmd(nc, [arrays], core_ids=[0])
    return r.results[0]["out"]
```

```python
from contextlib import ExitStack

import numpy as np
import concourse.bass as bass
import concourse.mybir as mybir

F32 = mybir.dt.float32
F32R = mybir.dt.float32r
I32 = mybir.dt.int32
ALU = mybir.AluOpType
ACT = mybir.ActivationFunctionType
AX = mybir.AxisListType
RMAX = bass.bass_isa.ReduceOp.max
RADD = bass.bass_isa.ReduceOp.add

P = 128
B, N, C = 2, 2048, 256
TB = N // P
NT = B * TB
KC = C // P
E, K, H = 8, 2, 192
F = 2 * H
HS = 384
MC = HS // P
G = 4
GT = G * P
NG = NT // G
NP = NG // 2
EPS = 1e-5
SCALE = float(C) ** -0.5
CAP = B * N + P
BLOCKS = (K * B * N + E * (P - 1)) // P
NBK = -(-BLOCKS // 4) * 4
AHEAD = 3
IDLE = 8
ROWS = E * CAP + IDLE * P
HR = H - P


def post_norm_layer(nc, x, w_qkv, w_kv_t, w_conv, gate_t, w1_t, w2_t, ws1_t, ws2_t, out):
    rows_in = nc.dram_tensor("rows_in", [ROWS, C], F32, kind="Internal").ap()
    rows_out = nc.dram_tensor("rows_out", [NBK * P, C], F32, kind="Internal").ap()

    with ExitStack() as ctx:
        def sb(name, shape, dt=F32):
            return ctx.enter_context(nc.sbuf_tensor(name, shape, dt))

        def sem(name):
            return ctx.enter_context(nc.semaphore(name))

        def pair(name):
            return [sem(f"{name}_even"), sem(f"{name}_odd")]

        xs = sb("xs", [P, NT, C])
        w1hi, w1lo = (sb(f"w1{n}", [P, E, KC, F], F32R) for n in ("hi", "lo"))
        w2hi, w2lo = (sb(f"w2{n}", [P, E, C], F32R) for n in ("hi", "lo"))
        w2rhi, w2rlo = (sb(f"w2r{n}", [P, E, C], F32R) for n in ("hi", "lo"))
        ws1hi, ws1lo = (sb(f"ws1{n}", [P, KC, 2 * HS], F32R) for n in ("hi", "lo"))
        ws2hi, ws2lo = (sb(f"ws2{n}", [P, MC, C], F32R) for n in ("hi", "lo"))
        x2 = [sb(f"x2_{n}", [P, G, C]) for n in range(2)]
        xthi, xtlo = (sb(f"xt{n}", [P, KC, GT], F32R) for n in ("hi", "lo"))
        hthi, htlo = (sb(f"ht{n}", [P, MC, GT], F32R) for n in ("hi", "lo"))
        mix = sb("mix", [P, 4, GT])
        stage = sb("stage", [P, 2, 3072])
        bxhi, bxlo = ([sb(f"bx{n}{i}", [P, KC, P], F32R) for i in range(2)] for n in ("hi", "lo"))
        bhhi = [sb(f"bhhi{i}", [P, 2, P], F32R) for i in range(2)]
        bhlo = [sb(f"bhlo{i}", [P, P], F32R) for i in range(2)]
        ones = sb("ones", [P, P])
        ident = sb("ident", [P, P])
        tri = sb("tri", [P, P])
        gatef = sb("gatef", [P, KC, E])
        gate = sb("gate", [P, KC, 2, E], F32R)
        wcol = sb("wcol", [P, KC])
        epst = sb("epst", [P, 1])
        agent = sb("agent", [P, B, TB])
        tok = sb("tok", [P, B, TB])
        tok2 = sb("tok2", [P, B, TB])
        lv = sb("lv", [P, B, TB])
        att = sb("att", [P, C])
        small = sb("small", [P, B, 8])
        bst = sb("bst", [P, G, 6])
        mv = sb("mv", [P, NT, 2])
        rstd = sb("rstd", [P, NT])
        rn = sb("rn", [P, 3, TB])
        fmv = sb("fmv", [P, G, 2])
        frn = sb("frn", [P, 4, G])
        top = sb("top", [P, NT, K])
        slot = sb("slot", [P, NT, K], I32)
        eid = sb("eid", [P, NT, K])
        place = sb("place", [P, NT, K], I32)
        rt = sb("rt", [P, 9, G, E])
        r4 = sb("r4", [P, 3, G])
        seen = sb("seen", [P, E])
        ebase = sb("ebase", [P, E])
        jota = sb("jota", [1, NBK])
        thr = sb("thr", [P, NT])
        te = sb("te", [1, 2, NBK])
        tc = sb("tc", [P, 6, E])
        clear = sb("clear", [P, C])
        m8 = sb("m8", [P, G, 8])
        i8 = sb("i8", [P, G, 8], mybir.dt.uint32)
        eota = sb("eota", [P, E])
        zrow = sb("zrow", [1, E], I32)
        brow = sb("brow", [1, NBK], I32)
        bexp = sb("bexp", [1, NBK], I32)
        banks = [ctx.enter_context(nc.psum_tensor(f"bank{n}", [P, 512], F32)) for n in range(8)]

        wq = mix[:, 0, :].rearrange("p (k c) -> p k c", k=KC)
        wv = mix[:, 1, :].rearrange("p (k c) -> p k c", k=KC)
        wkvt = mix[:, 2:4, :]
        sg = [mix[:, n, :] for n in range(2)]
        prod = [mix[:, 2 + n, :] for n in range(2)]
        wide = x2[0]
        junk = x2[1]
        flat = stage[:, 0, :]
        xg = [flat[:, n * C:(n + 1) * C] for n in range(4)]
        bsg = [flat[:, 1024 + n * H:1024 + (n + 1) * H] for n in range(2)]
        bprod = [flat[:, 1408 + n * 2 * P:1408 + (n + 1) * 2 * P] for n in range(2)]
        by = [flat[:, 1920 + n * C:1920 + (n + 1) * C] for n in range(4)]
        got = [[stage[:, k, n * G * C:(n + 1) * G * C].rearrange("p (t c) -> p t c", t=G) for n in range(2)]
               for k in range(K)]
        mvf = mv[:].rearrange("p t s -> p (t s)")
        topf = top[:].rearrange("p t k -> p (t k)")
        tokf = tok[:].rearrange("p b t -> p (b t)")
        agentf = agent[:].rearrange("p b t -> p (b t)")
        lvf = lv[:].rearrange("p b t -> p (b t)")

        bank_x, bank_y, bank_h, bank_t = banks[0:2], banks[2:4], banks[4:6], banks[6:8]

        s_x = [sem(f"x_loaded{b}") for b in range(B)]
        s_wq, s_wkv, s_gate = sem("wq_loaded"), sem("wkv_loaded"), sem("gate_loaded")
        s_raw = [sem(f"raw_loaded{n}") for n in range(5)]
        s_whi, s_wlo, s_gset = sem("weights_hi"), sem("weights_lo"), sem("gate_split")
        s_mem, s_set = sem("cleared"), sem("constants")
        s_pad = sem("padding_written")
        s_dve, s_pe, s_act, s_pool = sem("att_vector"), sem("att_tensor"), sem("att_scalar"), sem("att_pool")
        s_ag, s_lv, s_add, s_stat, s_agg = sem("agent"), sem("token_logits"), sem("att_added"), sem("ln1_sums"), sem("ln1_stats")

        s_x2, s_xtp, s_xhi, s_xt = sem("x2"), sem("x2t_psum"), sem("x2t_hi"), sem("x2t")
        s_lg, s_sh, s_ex, s_m = sem("logits"), sem("logits_shifted"), sem("exps"), sem("chosen")
        s_pos, s_slot, s_sc = sem("positions"), sem("slots"), pair("scattered")
        (s_lsum, s_lmax, s_esum, s_rcp, s_score, s_top8, s_idx, s_sel, s_place, s_tmp) = (
            sem(f"route_{n}") for n in ("logits", "max", "sum", "reciprocal", "scores", "top8", "index", "masks",
                                        "places", "terms"))
        s_h = [sem(f"hidden_psum{m}") for m in range(MC)]
        s_sg = [sem(f"silu{m}") for m in range(MC)]
        s_pr = [sem(f"product{m}") for m in range(MC)]
        s_hhi = [sem(f"hidden_hi{m}") for m in range(MC)]
        s_ht = sem("hidden")
        s_z = [sem(f"shared_psum{u}") for u in range(2)]
        s_zev = [sem(f"shared_added{u}") for u in range(2)]
        s_cnt, s_tb, s_tbl = sem("counts"), sem("table_steps"), sem("block_table")
        s_place_out = sem("result_places")

        s_ld = [sem(f"rows_loaded{n}") for n in range(4)]
        s_bxp, s_bxhi, s_bx = pair("rows_t_psum"), pair("rows_t_hi"), pair("rows_t")
        s_bh, s_bsg, s_bpr = pair("expert_hidden"), pair("expert_silu"), pair("expert_product")
        s_bhp, s_bhhi, s_bht = pair("expert_ht_psum"), pair("expert_ht_hi"), pair("expert_ht")
        s_by, s_byev, s_st = pair("expert_out"), pair("expert_row"), pair("rows_stored")

        s_got, s_first, s_sum = pair("gathered"), sem("first_added"), sem("summed")
        s_bst, s_var, s_std = sem("ln2_sums"), sem("ln2_stats"), sem("ln2_std")
        s_n = [sem(f"ln2_newton{n}") for n in range(5)]
        s_fin, s_out, s_tick = sem("ln2_ready"), pair("out_stored"), sem("wait_taken")

        block = ctx.enter_context(nc.Block())

        DVE = ["tok_shift", "g", "max", "tok_rcp", "sum_rcp", "att", "tok", "col", "lmax", "lneg", "psum_rcp", "s",
               "std_rcp", "square", "times_var", "newton", "rstd"]
        PE = ["g", "logits", "col", "r", "s", "value"]
        SCALAR = ["tok_exp", "exp", "p", "std"]
        POOL = ["max", "sum"]

        def dve(b, name):
            return 2 + b * len(DVE) + DVE.index(name)

        def pe_at(b, name):
            return 2 + b * len(PE) + PE.index(name)

        def act_at(b, name):
            return 1 + b * len(SCALAR) + SCALAR.index(name)

        def pool_at(b, name):
            return 1 + b * len(POOL) + POOL.index(name)

        def sl(start, size=1):
            return slice(start, start + size) if isinstance(start, int) else bass.ds(start, size)

        def groups(eng, body):
            for n in (1, 2):
                body(n, (n - 1) % 2)
            with eng.Fori(2, NP) as i:
                body(eng.snap(2 * i - 1), 0)
                body(eng.snap(2 * i), 1)
            for n in (NG - 1, NG):
                body(n, (n - 1) % 2)

        def later(n, by=1):
            return not isinstance(n, int) or n > by

        def more(n):
            return not isinstance(n, int) or n < NG

        def nth(n, of, k):
            return (n - 1) * of + k + 1

        def blocks(eng, step):
            def static(j):
                def at(d):
                    b = j + d
                    return (b // 2 + 1, b % 2, b // 4 + 1, b % 4) if 0 <= b < NBK else None
                return at
            for j in range(-AHEAD, 8):
                step(static(j))
            with eng.Fori(2, NBK // 4 - 1) as i:
                known = {}

                def count(times, off):
                    if (times, off) not in known:
                        known[times, off] = eng.snap(times * i + off)
                    return known[times, off]

                for o in range(4):
                    step(lambda d, o=o: (count(2, (o + d) // 2 + 1), (o + d) % 2, count(1, (o + d) // 4 + 1), (o + d) % 4))
            for j in range(NBK - 4, NBK + 2):
                step(static(j))

        def block_id(c, par):
            return sl((c - 1) * 2 + par)

        S1 = KC * 2 * HS
        RAW = [stage[:, 0, 0:S1 + MC * C], stage[:, 1, 0:4 * KC * F], stage[:, 0, 0:4 * KC * F],
               stage[:, 1, 0:E * C], stage[:, 0, 0:E * C]]

        def parts(s1, s2, a, b, r):
            return [[(s1[:].rearrange("p k f -> p (k f)"), RAW[0][:, 0:S1]),
                     (s2[:].rearrange("p m c -> p (m c)"), RAW[0][:, S1:])],
                    [(a[:, 0:4].rearrange("p e k f -> p (e k f)"), RAW[1])],
                    [(a[:, 4:8].rearrange("p e k f -> p (e k f)"), RAW[2])],
                    [(b[:].rearrange("p e c -> p (e c)"), RAW[3])],
                    [(r[:].rearrange("p e c -> p (e c)"), RAW[4])]]

        HI = parts(ws1hi, ws2hi, w1hi, w2hi, w2rhi)
        LO = parts(ws1lo, ws2lo, w1lo, w2lo, w2rlo)
        SPLIT = [2, 3, 4, 5, 6]

        @block.sync
        def _(sp):
            sp.dma_start(xs[:, 0:TB, :], x[0].rearrange("(p j) c -> p j c", j=TB)).then_inc(s_x[0], 16)
            sp.dma_start(wq, w_qkv[0:C].rearrange("(k p) c -> p k c", p=P)).then_inc(s_wq, 16)
            sp.dma_start(wcol[:], w_conv).then_inc(s_wq, 16)
            sp.dma_start(wkvt, w_kv_t.rearrange("(k p) c -> p k c", p=P)).then_inc(s_wkv, 16)
            sp.dma_start(wv, w_qkv[2 * C:3 * C].rearrange("(k p) c -> p k c", p=P)).then_inc(s_wkv, 16)
            sp.dma_start(xs[:, TB:NT, :], x[1].rearrange("(p j) c -> p j c", j=TB)).then_inc(s_x[1], 16)
            sp.dma_start(gatef[:], gate_t.rearrange("(k p) e -> p k e", p=P)).then_inc(s_gate, 16)
            sp.dma_start(RAW[0][:, 0:S1].rearrange("p (k f) -> p k f", k=KC),
                         ws1_t.rearrange("(k p) f -> p k f", p=P)).then_inc(s_raw[0], 16)
            sp.dma_start(RAW[0][:, S1:].rearrange("p (m c) -> p m c", m=MC),
                         ws2_t.rearrange("(m p) c -> p m c", p=P)).then_inc(s_raw[0], 16)
            for n in range(2):
                if n == 1:
                    sp.wait_ge(s_whi, SPLIT[0])
                    sp.wait_ge(s_wlo, SPLIT[0])
                for e in range(4):
                    sp.dma_start(RAW[1 + n].rearrange("p (e k f) -> p e k f", e=4, k=KC)[:, e],
                                 w1_t[4 * n + e].rearrange("(k p) f -> p k f", p=P)).then_inc(s_raw[1 + n], 16)
            sp.wait_ge(s_whi, SPLIT[1])
            sp.wait_ge(s_wlo, SPLIT[1])
            sp.dma_start(RAW[3].rearrange("p (e c) -> p e c", e=E),
                         w2_t[:, 0:P].rearrange("e p c -> p e c")).then_inc(s_raw[3], 16)
            sp.wait_ge(s_whi, SPLIT[2])
            sp.wait_ge(s_wlo, SPLIT[2])
            for n in range(2):
                sp.dma_start(RAW[4][n * HR:(n + 1) * HR].rearrange("p (e c) -> p e c", e=E),
                             w2_t[:, P:H].rearrange("e p c -> p e c")).then_inc(s_raw[4], 16)
            sp.wait_ge(s_mem, 2)
            for n in range(IDLE):
                sp.dma_start(rows_in[E * CAP + n * P:E * CAP + (n + 1) * P, :], clear[:]).then_inc(s_pad, 16)
            sp.wait_ge(s_tbl, 1)
            for e in range(E):
                r = sp.value_load(zrow[0:1, e:e + 1], min_val=0, max_val=ROWS - P)
                sp.dma_start(rows_in[bass.ds(r, P), :], clear[:]).then_inc(s_pad, 16)
            for n in range(2):
                sp.wait_ge(s_sc[n], 16 * K * G * NP)
            sp.wait_ge(s_pad, 16 * (IDLE + E))
            sp.wait_ge(s_whi, SPLIT[4])
            sp.wait_ge(s_wlo, SPLIT[4])

            def step(at):
                if load := at(AHEAD):
                    c, par, quad, buf = load
                    if not (isinstance(c, int) and c <= 2):
                        sp.wait_ge(s_bxp[par], c - 2)
                    r = sp.value_load(brow[0:1, block_id(c, par)], min_val=0, max_val=ROWS - P)
                    sp.dma_start(xg[buf], rows_in[bass.ds(r, P), :]).then_inc(s_ld[buf], 16)
                store = at(-2)
                if store and store[1] == 1:
                    c, par, quad, buf = store
                    for n in range(2):
                        sp.wait_ge(s_byev[n], c)
                    sp.dma_start(rows_out[sl((c - 1) * 2 * P, 2 * P), :].rearrange("(n p) c -> p n c", n=2),
                                 flat[:, 1920 + (buf - 1) * C:1920 + (buf + 1) * C].rearrange("p (n c) -> p n c", n=2)
                                 ).then_inc(s_st[buf // 2], 16)

            blocks(sp, step)
            for q in range(NG):
                sp.wait_ge(s_fin, q + 1)
                n = q * G
                sp.dma_start(out[n // TB].rearrange("(p j) c -> p j c", j=TB)[:, n % TB:n % TB + G, :],
                             got[0][q % 2]).then_inc(s_out[q % 2], 16)
            for par in range(2):
                sp.wait_ge(s_out[par], 16 * NP)

        @block.gpsimd
        def _(pool):
            pool.memset(ones[:], 1.0).then_inc(s_mem, 1)
            pool.memset(ident[:], 0.0)
            pool.memset(epst[:], EPS)
            pool.memset(seen[:], 0.0)
            pool.memset(tri[:], 1.0)
            pool.memset(clear[:], 0.0).then_inc(s_mem, 1)
            pool.wait_ge(s_mem, 2)
            pool.affine_select(out=ident[:], in_=ident[:], compare_op=ALU.not_equal, fill=1.0, base=0,
                               pattern=[[-1, P]], channel_multiplier=1)
            pool.affine_select(out=tri[:], in_=tri[:], compare_op=ALU.is_gt, fill=0.0, base=0,
                               pattern=[[1, P]], channel_multiplier=-1)
            pool.iota(ebase[:], [[CAP, E]], base=0, channel_multiplier=0, allow_small_or_imprecise_dtypes=True)
            pool.iota(eota[:], [[1, E]], base=0, channel_multiplier=0, allow_small_or_imprecise_dtypes=True)
            pool.iota(jota[:], [[1, NBK]], base=0, channel_multiplier=0, allow_small_or_imprecise_dtypes=True)
            pool.iota(thr[:], [[P, NT]], base=0, channel_multiplier=0,
                      allow_small_or_imprecise_dtypes=True).then_inc(s_set, 1)

            def low(n):
                for m, (dst, src) in enumerate(LO[n]):
                    pool.wait_ge(s_whi, SPLIT[n])
                    pool.tensor_tensor(dst, src, HI[n][m][0].bitcast(F32), ALU.subtract).then_inc(s_wlo, 1)

            low(0)
            for b in range(B):
                pool.wait_ge(s_dve, dve(b, "lmax"))
                pool.partition_all_reduce(small[:, b, 3:4], small[:, b, 2:3], P, RMAX).then_inc(s_pool, 1)
                pool.wait_ge(s_act, act_at(b, "p"))
                pool.partition_all_reduce(small[:, b, 6:7], small[:, b, 5:6], P, RADD).then_inc(s_pool, 1)
            for n in range(1, 5):
                low(n)
            for q in range(NG):
                pool.wait_ge(s_slot, q + 1)
                for t in range(G):
                    for k in range(K):
                        pool.indirect_dma_start(
                            rows_in[0:E * CAP, :], bass.IndirectOffsetOnAxis(slot[:, q * G + t, k:k + 1], 0),
                            x2[q % 2][:, t, :], None).then_inc(s_sc[q % 2], 16)
            for n in range(2):
                pool.wait_ge(s_st[n], 16 * (NBK // 4))
            pool.wait_ge(s_place_out, 1)
            for q in range(NG):
                if q >= 2:
                    pool.wait_ge(s_out[q % 2], 16 * (q // 2))
                for t in range(G):
                    for k in range(K):
                        pool.indirect_dma_start(
                            got[k][q % 2][:, t, :], None, rows_out[:, :],
                            bass.IndirectOffsetOnAxis(place[:, q * G + t, k:k + 1], 0)).then_inc(s_got[q % 2], 16)

        @block.scalar
        def _(act):
            def high(n, dmas):
                act.wait_ge(s_raw[n], 16 * dmas)
                for dst, src in HI[n]:
                    act.activation(dst, src, ACT.Copy).then_inc(s_whi, 1)

            high(0, 2)
            for b in range(B):
                act.wait_ge(s_dve, dve(b, "tok_shift"))
                act.activation(tok[:, b, :], tok2[:, b, :], ACT.Exp).then_inc(s_act, 1)
                act.wait_ge(s_dve, dve(b, "max"))
                act.activation(att[:], banks[2][:, b * C:(b + 1) * C], ACT.Exp, bias=small[:, b, 0:1],
                               accum_out=small[:, b, 1:2]).then_inc(s_act, 1)
                act.wait_ge(s_dve, dve(b, "lneg"))
                act.activation(lv[:, b, :], lv[:, b, :], ACT.Exp, bias=small[:, b, 4:5],
                               accum_out=small[:, b, 5:6]).then_inc(s_act, 1)
                high(1 + b, 4)
                act.wait_ge(s_agg, NP * (b + 1))
                act.activation(rn[:, 0, :], mv[:, b * TB:(b + 1) * TB, 1], ACT.Sqrt, bias=epst[:]).then_inc(s_act, 1)
            high(3, 1)
            high(4, 2)

            def rows_hi(n):
                if later(n):
                    act.wait_ge(s_h[MC - 1], n - 1)
                for k in range(KC):
                    act.wait_ge(s_xtp, nth(n, KC, k))
                    act.activation(xthi[:, k, :], banks[k][:], ACT.Copy).then_inc(s_xhi, 1)

            def group(n, par):
                act.wait_ge(s_sh, n)
                act.activation(rt[:, 2], rt[:, 1], ACT.Exp).then_inc(s_ex, 1)
                act.preload_act_table(ACT.Silu)
                for m in range(MC):
                    buf = (par + m) % 2
                    act.wait_ge(s_h[m], n)
                    act.activation(sg[buf], banks[5 + 2 * buf][:], ACT.Silu).then_inc(s_sg[m], 1)
                    if m == 0 and later(n):
                        act.wait_ge(s_z[1], n - 1)
                    act.wait_ge(s_pr[m], n)
                    act.activation(hthi[:, m, :], prod[buf], ACT.Copy).then_inc(s_hhi[m], 1)
                if more(n):
                    rows_hi(n + 1)
                    act.preload_act_table(ACT.Exp)

            rows_hi(1)
            act.preload_act_table(ACT.Exp)
            groups(act, group)
            act.preload_act_table(ACT.Silu)

            def step(at):
                if rows := at(1):
                    c, par, _, _ = rows
                    act.wait_ge(s_bxp[par], c)
                    act.activation(bxhi[par][:].rearrange("p k t -> p (k t)"), bank_x[par][:, 0:C],
                                   ACT.Copy).then_inc(s_bxhi[par], 1)
                if now := at(0):
                    c, par, _, _ = now
                    act.wait_ge(s_bh[par], c)
                    act.activation(bsg[par], bank_h[par][:, H:F], ACT.Silu).then_inc(s_bsg[par], 1)
                if hidden := at(-1):
                    c, par, _, _ = hidden
                    act.wait_ge(s_bhp[par], c)
                    act.activation(bhhi[par][:].rearrange("p k t -> p (k t)"), bank_t[par][:, 0:2 * P],
                                   ACT.Copy).then_inc(s_bhhi[par], 1)
                if result := at(-2):
                    c, par, quad, buf = result
                    act.wait_ge(s_by[par], c)
                    if not (isinstance(quad, int) and quad == 1):
                        act.wait_ge(s_st[buf // 2], 16 * (quad - 1))
                    act.activation(by[buf], bank_y[par][:, 0:C], ACT.Copy).then_inc(s_byev[par], 1)

            blocks(act, step)
            act.preload_act_table(ACT.Sqrt)
            with act.Fori(1, NG + 1) as n:
                act.wait_ge(s_var, n)
                act.activation(frn[:, 0, :], fmv[:, :, 1], ACT.Sqrt, bias=epst[:]).then_inc(s_std, 1)

        @block.tensor
        def _(pe):
            pe.wait_ge(s_wq, 32)
            pe.wait_ge(s_dve, 1)
            for k in range(KC):
                mm = pe.matmul(banks[0][:, 0:C], wide[:, 0, k * P:(k + 1) * P], wq[:, k, :],
                               start=(k == 0), stop=(k == KC - 1))
            mm.then_inc(s_pe, 1)

            def weighted_sum(bank, b, weight):
                for k in range(KC):
                    for t in range(TB):
                        mm = pe.matmul(bank[:, 8 * b + k:8 * b + k + 1], xs[:, b * TB + t, k * P:(k + 1) * P],
                                       weight[:, b, t:t + 1], start=(t == 0), stop=(t == TB - 1))
                return mm

            def with_matrix(bank, b, spread, matrix):
                for k in range(KC):
                    mm = pe.matmul(bank[:, b * C:(b + 1) * C], spread[:, 1 + b, k * P:(k + 1) * P], matrix(k),
                                   start=(k == 0), stop=(k == KC - 1))
                return mm

            for b in range(B):
                pe.wait_ge(s_ag, TB * (b + 1))
                weighted_sum(banks[1], b, agent).then_inc(s_pe, 1)
                pe.wait_ge(s_dve, dve(b, "g"))
                pe.wait_ge(s_wkv, 32)
                with_matrix(banks[2], b, wide, lambda k: wkvt[:, k, 0:C]).then_inc(s_pe, 1)
                pe.wait_ge(s_dve, dve(b, "att"))
                for k in range(KC):
                    mm = pe.matmul(banks[3][:, 8 * b + k:8 * b + k + 1], att[0:1, k * P:(k + 1) * P], ones[0:1, 0:1],
                                   start=True, stop=True)
                mm.then_inc(s_pe, 1)
                pe.wait_ge(s_dve, dve(b, "col"))
                with_matrix(banks[4], b, wide, lambda k: wv[:, k, :]).then_inc(s_pe, 1)
                pe.wait_ge(s_act, act_at(b, "p"))
                weighted_sum(banks[5], b, lv).then_inc(s_pe, 1)
                pe.wait_ge(s_dve, dve(b, "s"))
                with_matrix(banks[6], b, wide, lambda k: wkvt[:, k, C:2 * C]).then_inc(s_pe, 1)

            pe.wait_ge(s_set, 1)
            pe.wait_ge(s_gset, 2)
            pe.wait_ge(s_wlo, SPLIT[0])

            def transposes(n, par):
                pe.wait_ge(s_x2, n)
                for k in range(KC):
                    for t in range(G):
                        mm = pe.transpose(banks[k][:, t * P:(t + 1) * P], x2[par][:, t, k * P:(k + 1) * P], ident[:])
                    mm.then_inc(s_xtp, 1)

            def places(n):
                pe.wait_ge(s_m, n)
                chosen = rt[:, 7].rearrange("p t e -> p (t e)")
                pe.matmul(banks[2][:, 64:64 + G * E], tri[:], chosen, start=True, stop=False)
                for d in range(1, G):
                    pe.matmul(banks[2][:, 64 + d * E:64 + G * E], ones[:], chosen[:, 0:(G - d) * E],
                              start=False, stop=False)
                pe.matmul(banks[2][:, 64:64 + G * E].rearrange("p (t e) -> p t e", t=G), ones[:],
                          seen[:].unsqueeze(1).broadcast_to([P, G, E]), start=False, stop=True).then_inc(s_pos, 1)

            def group(n, par):
                if later(n):
                    pe.wait_ge(s_place, n - 1)
                pe.wait_ge(s_xt, n)
                for t in range(G):
                    steps = [(xt, k) for xt in (xthi, xtlo) for k in range(KC)]
                    for a, (xt, k) in enumerate(steps):
                        mm = pe.matmul(banks[2][:, t * 2 * E:(t + 1) * 2 * E], xt[:, k, t * P:(t + 1) * P],
                                       gate[:, k].rearrange("p h e -> p (h e)"),
                                       start=(a == 0), stop=(a == len(steps) - 1))
                mm.then_inc(s_lg, 1)
                for m in range(MC):
                    buf = (par + m) % 2
                    if m == 2:
                        pe.wait_ge(s_pr[0], n)
                    elif later(n):
                        pe.wait_ge(s_pr[m + 1], n - 1)
                        if m == 0:
                            pe.wait_ge(s_zev[0], n - 1)
                    for o, bank in ((m * P, banks[4 + 2 * buf]), (HS + m * P, banks[5 + 2 * buf])):
                        steps = [(w, xt, k) for w, xt in ((ws1hi, xthi), (ws1hi, xtlo), (ws1lo, xthi)) for k in range(KC)]
                        for a, (w, xt, k) in enumerate(steps):
                            mm = pe.matmul(bank[:], w[:, k, o:o + P], xt[:, k, :],
                                           start=(a == 0), stop=(a == len(steps) - 1))
                    mm.then_inc(s_h[m], 1)
                    if m == 1:
                        places(n)
                if more(n):
                    transposes(n + 1, 1 - par)
                pe.wait_ge(s_pr[1], n)
                for u, bank in enumerate((banks[4 + 2 * (1 - par)], banks[3])):
                    if u == 1 and later(n):
                        pe.wait_ge(s_zev[1], n - 1)
                    for t in (2 * u, 2 * u + 1):
                        for m in range(MC):
                            if t == 0:
                                pe.wait_ge(s_ht, nth(n, MC, m))
                            steps = [(hthi, ws2hi), (htlo, ws2hi), (hthi, ws2lo)]
                            for a, (ht, w) in enumerate(steps):
                                mm = pe.matmul(bank[:, (t % 2) * C:(t % 2 + 1) * C], ht[:, m, t * P:(t + 1) * P],
                                               w[:, m, :], start=(m == 0 and a == 0),
                                               stop=(m == MC - 1 and a == len(steps) - 1))
                    mm.then_inc(s_z[u], 1)

            transposes(1, 0)
            groups(pe, group)
            pe.wait_ge(s_slot, NG)
            pe.matmul(banks[2][:, 128:128 + E], ones[:], seen[:], start=True, stop=True).then_inc(s_cnt, 1)
            pe.wait_ge(s_tbl, 1)
            pe.wait_ge(s_wlo, SPLIT[4])

            def step(at):
                if rows := at(1):
                    c, par, quad, buf = rows
                    pe.wait_ge(s_ld[buf], 16 * quad)
                    for k in range(KC):
                        mm = pe.transpose(bank_x[par][:, k * P:(k + 1) * P], xg[buf][:, k * P:(k + 1) * P], ident[:])
                    mm.then_inc(s_bxp[par], 1)
                if now := at(0):
                    c, par, _, _ = now
                    e = pe.value_load(bexp[0:1, block_id(c, par)], min_val=0, max_val=E - 1)
                    pe.wait_ge(s_bx[par], c)
                    steps = [(bx, w, k) for bx, w in ((bxhi, w1hi), (bxlo, w1hi), (bxhi, w1lo)) for k in range(KC)]
                    for a, (bx, w, k) in enumerate(steps):
                        mm = pe.matmul(bank_h[par][:, 0:F], bx[par][:, k, :], w[:, bass.ds(e, 1), k, :],
                                       start=(a == 0), stop=(a == len(steps) - 1))
                    mm.then_inc(s_bh[par], 1)
                if hidden := at(-1):
                    c, par, _, _ = hidden
                    pe.wait_ge(s_bpr[par], c)
                    for k in range(2):
                        mm = pe.transpose(bank_t[par][:, k * P:(k + 1) * P], bprod[par][:, k * P:(k + 1) * P], ident[:])
                    mm.then_inc(s_bhp[par], 1)
                if result := at(-2):
                    c, par, _, _ = result
                    e = pe.value_load(bexp[0:1, block_id(c, par)], min_val=0, max_val=E - 1)
                    pe.wait_ge(s_bht[par], c)
                    if not (isinstance(c, int) and c == 1):
                        pe.wait_ge(s_byev[par], c - 1)
                    first, second = bhhi[par][:, 0, :], bhhi[par][:, 1, :]
                    steps = [(first, w2hi), (bhlo[par][:], w2hi), (first, w2lo), (second, w2rhi), (second, w2rlo)]
                    for a, (ht, w) in enumerate(steps):
                        mm = pe.matmul(bank_y[par][:, 0:C], ht, w[:, bass.ds(e, 1), :],
                                       start=(a == 0), stop=(a == len(steps) - 1))
                    mm.then_inc(s_by[par], 1)

            blocks(pe, step)

        @block.vector
        def _(vec):
            def spread(dst, col, b, scale):
                for k in range(KC):
                    ins = vec.tensor_scalar(dst[:, k * P:(k + 1) * P], ones[:], col[:, k:k + 1], scale, ALU.mult, ALU.mult)
                return ins

            vec.wait_ge(s_wq, 32)
            vec.wait_ge(s_mem, 1)
            spread(wide[:, 0, :], wcol, 0, 1.0).then_inc(s_dve, 1)
            vec.wait_ge(s_gate, 16)
            vec.tensor_copy(gate[:, :, 0, :], gatef[:]).then_inc(s_gset, 1)
            vec.wait_ge(s_gset, 1)
            vec.tensor_tensor(gate[:, :, 1, :], gatef[:], gate[:, :, 0, :].bitcast(F32), ALU.subtract).then_inc(s_gset, 1)

            def dots(row, dst, b, done):
                for t in range(b * TB, (b + 1) * TB):
                    if t >= G:
                        vec.wait_ge(done, t - G + 1)
                    vec.tensor_tensor_reduce(junk[:, t % G, :], xs[:, t, :], row, 1.0, 0.0, ALU.mult, ALU.add,
                                             dst[:, t:t + 1]).then_inc(done, 1)

            vec.wait_ge(s_pe, 1)
            for b in range(B):
                vec.wait_ge(s_x[b], 16)
                dots(banks[0][:, 0:C], agentf, b, s_ag)

            for b in range(B):
                c8 = slice(8 * b, 8 * b + KC)
                vec.wait_ge(s_ag, TB * (b + 1))
                vec.tensor_tensor(tok2[:, b, :], agent[:, b, :], agent[:, b, :], ALU.subtract).then_inc(s_dve, 1)
                vec.wait_ge(s_pe, pe_at(b, "g"))
                spread(wide[:, 1 + b, :], banks[1][:, c8], b, SCALE).then_inc(s_dve, 1)
                vec.wait_ge(s_pe, pe_at(b, "logits"))
                vec.tensor_reduce(small[:, b, 0:1], banks[2][:, b * C:(b + 1) * C], AX.X, ALU.max,
                                  negate=True).then_inc(s_dve, 1)
                vec.wait_ge(s_act, act_at(b, "tok_exp"))
                vec.reciprocal(tok2[:, b, :], tok[:, b, :]).then_inc(s_dve, 1)
                vec.wait_ge(s_act, act_at(b, "exp"))
                vec.reciprocal(small[:, b, 7:8], small[:, b, 1:2]).then_inc(s_dve, 1)
                vec.wait_ge(s_dve, dve(b, "sum_rcp"))
                vec.tensor_scalar(att[0:1, :], att[0:1, :], small[0:1, b, 7:8], None, ALU.mult).then_inc(s_dve, 1)
                vec.tensor_tensor(tok[:, b, :], tok[:, b, :], tok2[:, b, :], ALU.mult).then_inc(s_dve, 1)
                vec.wait_ge(s_pe, pe_at(b, "col"))
                spread(wide[:, 1 + b, :], banks[3][:, c8], b, 1.0).then_inc(s_dve, 1)
                vec.wait_ge(s_pe, pe_at(b, "r"))
                dots(banks[4][:, b * C:(b + 1) * C], lvf, b, s_lv)
                vec.wait_ge(s_lv, TB * (b + 1))
                vec.tensor_reduce(small[:, b, 2:3], lv[:, b, :], AX.X, ALU.max).then_inc(s_dve, 1)
                vec.wait_ge(s_pool, pool_at(b, "max"))
                vec.tensor_scalar(small[:, b, 4:5], small[:, b, 3:4], -1.0, None, ALU.mult).then_inc(s_dve, 1)
                vec.wait_ge(s_pool, pool_at(b, "sum"))
                vec.reciprocal(small[:, b, 7:8], small[:, b, 6:7]).then_inc(s_dve, 1)
                vec.wait_ge(s_pe, pe_at(b, "s"))
                vec.wait_ge(s_dve, dve(b, "psum_rcp"))
                spread(wide[:, 1 + b, :], banks[5][:, c8], b, small[:, b, 7:8]).then_inc(s_dve, 1)
                vec.wait_ge(s_pe, pe_at(b, "value"))
                for g in range(b * NP, (b + 1) * NP):
                    for t in range(g * G, (g + 1) * G):
                        ins = vec.scalar_tensor_tensor(xs[:, t, :], banks[6][:, b * C:(b + 1) * C], tokf[:, t:t + 1],
                                                       xs[:, t, :], ALU.mult, ALU.add)
                    ins.then_inc(s_add, 1)
                    vec.wait_ge(s_add, g + 1)
                    for t in range(G):
                        ins = vec.bn_stats(bst[:, t, :], xs[:, g * G + t, :])
                    ins.then_inc(s_stat, 1)
                    vec.wait_ge(s_stat, g + 1)
                    for t in range(G):
                        ins = vec.bn_aggr(mv[:, g * G + t, :], bst[:, t, :])
                    ins.then_inc(s_agg, 1)
                var = mv[:, b * TB:(b + 1) * TB, 1]
                vec.wait_ge(s_act, act_at(b, "std"))
                vec.reciprocal(rn[:, 1, :], rn[:, 0, :]).then_inc(s_dve, 1)
                vec.wait_ge(s_dve, dve(b, "std_rcp"))
                vec.tensor_tensor(rn[:, 2, :], rn[:, 1, :], rn[:, 1, :], ALU.mult).then_inc(s_dve, 1)
                vec.wait_ge(s_dve, dve(b, "square"))
                vec.scalar_tensor_tensor(rn[:, 2, :], var, EPS, rn[:, 2, :], ALU.add, ALU.mult).then_inc(s_dve, 1)
                vec.wait_ge(s_dve, dve(b, "times_var"))
                vec.tensor_scalar(rn[:, 2, :], rn[:, 2, :], -0.5, 1.5, ALU.mult, ALU.add).then_inc(s_dve, 1)
                vec.wait_ge(s_dve, dve(b, "newton"))
                vec.tensor_tensor(rstd[:, b * TB:(b + 1) * TB], rn[:, 1, :], rn[:, 2, :], ALU.mult).then_inc(s_dve, 1)

            vec.wait_ge(s_dve, dve(B - 1, "rstd"))
            vec.wait_ge(s_set, 1)

            def normalise(n, par):
                tile = (n - 1) * G if isinstance(n, int) else vec.snap((n - 1) * G)
                if later(n, 2):
                    vec.wait_ge(s_sc[par], (n - 1 - par) * (16 * K * G // 2))
                for t in range(G):
                    ins = vec.tensor_scalar(x2[par][:, t:t + 1, :], xs[:, sl(tile + t), :], mvf[:, sl(2 * (tile + t))],
                                            rstd[:, sl(tile + t)], ALU.subtract, ALU.mult)
                ins.then_inc(s_x2, 1)

            def rows_lo(n):
                for k in range(KC):
                    vec.wait_ge(s_xhi, nth(n, KC, k))
                    ins = vec.tensor_tensor(xtlo[:, k, :], banks[k][:], xthi[:, k, :].bitcast(F32), ALU.subtract)
                ins.then_inc(s_xt, 1)

            def route(n, tile):
                vec.wait_ge(s_lg, n)
                vec.tensor_reduce(rt[:, 0], banks[2][:, 0:2 * G * E].rearrange("p (t h e) -> p t e h", t=G, h=2), AX.X,
                                  ALU.add).then_inc(s_lsum, 1)
                vec.wait_ge(s_lsum, n)
                vec.tensor_reduce(r4[:, 0], rt[:, 0], AX.X, ALU.max).then_inc(s_lmax, 1)
                vec.wait_ge(s_lmax, n)
                vec.tensor_tensor(rt[:, 1], rt[:, 0], r4[:, 0].unsqueeze(2).broadcast_to([P, G, E]),
                                  ALU.subtract).then_inc(s_sh, 1)
                vec.wait_ge(s_ex, n)
                vec.tensor_reduce(r4[:, 1], rt[:, 2], AX.X, ALU.add).then_inc(s_esum, 1)
                vec.wait_ge(s_esum, n)
                vec.reciprocal(r4[:, 2], r4[:, 1]).then_inc(s_rcp, 1)
                vec.wait_ge(s_rcp, n)
                vec.tensor_tensor(rt[:, 3], rt[:, 2], r4[:, 2].unsqueeze(2).broadcast_to([P, G, E]),
                                  ALU.mult).then_inc(s_score, 1)
                vec.wait_ge(s_score, n)
                vec.sem_inc(s_tick, 1)
                for t in range(G):
                    ins = vec.max(m8[:, t, :], rt[:, 3, t, :])
                ins.then_inc(s_top8, 1)
                vec.wait_ge(s_top8, n)
                vec.sem_inc(s_tick, 1)
                for t in range(G):
                    ins = vec.max_index(i8[:, t, :], m8[:, t, :], rt[:, 3, t, :])
                ins.then_inc(s_idx, 1)
                vec.tensor_copy(top[:, sl(tile, G), :], m8[:, :, 0:K])
                vec.wait_ge(s_idx, n)
                for k in range(K):
                    ins = vec.tensor_tensor(rt[:, 5 + k], eota[:].unsqueeze(1).broadcast_to([P, G, E]),
                                            i8[:, :, k:k + 1].broadcast_to([P, G, E]), ALU.is_equal)
                ins.then_inc(s_sel, 1)
                vec.tensor_copy(eid[:, sl(tile, G), :], i8[:, :, 0:K])
                vec.wait_ge(s_sel, n)
                vec.tensor_tensor(rt[:, 7], rt[:, 5], rt[:, 6], ALU.add).then_inc(s_m, 1)

            def slots(n, tile):
                vec.wait_ge(s_pos, n)
                vec.tensor_tensor(rt[:, 8], banks[2][:, 64:64 + G * E].rearrange("p (t e) -> p t e", t=G),
                                  ebase[:].unsqueeze(1).broadcast_to([P, G, E]), ALU.add).then_inc(s_place, 1)
                vec.tensor_reduce(rt[:, 4, 0, :], rt[:, 7].rearrange("p t e -> p e t"), AX.X, ALU.add)
                vec.wait_ge(s_place, n)
                for k in range(K):
                    ins = vec.tensor_tensor(rt[:, 5 + k], rt[:, 5 + k], rt[:, 8], ALU.mult)
                ins.then_inc(s_tmp, 1)
                vec.wait_ge(s_tmp, n)
                vec.tensor_tensor(seen[:], seen[:], rt[:, 4, 0, :], ALU.add)
                for k in range(K):
                    with nc.allow_low_precision(reason="row numbers below 2**24: exact"):
                        ins = vec.tensor_reduce(slot[:, sl(tile, G), k:k + 1], rt[:, 5 + k], AX.X, ALU.add)
                ins.then_inc(s_slot, 1)

            def group(n, par):
                tile = (n - 1) * G if isinstance(n, int) else vec.snap((n - 1) * G)
                route(n, tile)
                for m in range(MC):
                    buf = (par + m) % 2
                    if m == 2:
                        slots(n, tile)
                    vec.wait_ge(s_sg[m], n)
                    vec.tensor_tensor(prod[buf], banks[4 + 2 * buf][:], sg[buf], ALU.mult).then_inc(s_pr[m], 1)
                    vec.wait_ge(s_hhi[m], n)
                    vec.tensor_tensor(htlo[:, m, :], prod[buf], hthi[:, m, :].bitcast(F32), ALU.subtract).then_inc(s_ht, 1)
                    if m == 0 and more(n):
                        normalise(n + 1, 1 - par)
                if more(n):
                    rows_lo(n + 1)
                for u, bank in enumerate((banks[4 + 2 * (1 - par)], banks[3])):
                    vec.wait_ge(s_z[u], n)
                    vec.tensor_tensor(xs[:, sl(tile + 2 * u, 2), :], bank[:].rearrange("p (t c) -> p t c", t=2),
                                      x2[par][:, 2 * u:2 * u + 2, :], ALU.add).then_inc(s_zev[u], 1)

            normalise(1, 0)
            rows_lo(1)
            groups(vec, group)

            steps = [0]

            def table(ins):
                steps[0] += 1
                ins.then_inc(s_tb, 1)
                vec.wait_ge(s_tb, steps[0])

            count, nblk, last, unit, shift = (tc[:, n, :] for n in range(5))
            bid, start = te[:, 0, :], te[:, 1, :]
            space = stage[:, 1, :]
            grid = [space[0:1, n * NBK * E:(n + 1) * NBK * E].rearrange("p (j e) -> p j e", e=E) for n in range(2)]
            over = space[:, 2 * NBK * E:2 * NBK * E + E * NT].rearrange("p (e t) -> p e t", e=E)
            own = [space[:, 1408 + n * NT * K * E:1408 + (n + 1) * NT * K * E].rearrange("p (s e) -> p s e", e=E)
                   for n in range(2)]
            flat_k = [a[:].rearrange("p t k -> p (t k)") for a in (eid, slot, place)]
            vec.wait_ge(s_cnt, 1)
            vec.wait_ge(s_wlo, SPLIT[4])
            vec.memset(unit, 1.0)
            table(vec.tensor_copy(count, banks[2][:, 128:128 + E]))
            vec.tensor_tensor(zrow[:], count[0:1, :], ebase[0:1, :], ALU.add)
            table(vec.tensor_tensor(over, thr[:].unsqueeze(1).broadcast_to([P, E, NT]),
                                    count.unsqueeze(2).broadcast_to([P, E, NT]), ALU.is_lt))
            table(vec.tensor_reduce(nblk, over, AX.X, ALU.add))
            table(vec.tensor_tensor_scan(last, unit, nblk, 0.0, ALU.mult, ALU.add))
            table(vec.tensor_tensor(grid[0], jota[:].unsqueeze(2).broadcast_to([1, NBK, E]),
                                    last[0:1, :].unsqueeze(1).broadcast_to([1, NBK, E]), ALU.is_ge))
            table(vec.tensor_tensor(grid[1], grid[0], nblk[0:1, :].unsqueeze(1).broadcast_to([1, NBK, E]), ALU.mult))
            vec.tensor_reduce(bid, grid[0], AX.X, ALU.add)
            table(vec.tensor_reduce(start, grid[1], AX.X, ALU.add))
            vec.tensor_scalar(bexp[:], bid, float(E - 1), None, ALU.min)
            table(vec.tensor_tensor(start, jota[:], start, ALU.subtract))
            table(vec.tensor_scalar(bid, bid, float(CAP), None, ALU.mult))
            table(vec.scalar_tensor_tensor(brow[:], start, float(P), bid, ALU.mult, ALU.add))
            vec.engine_nop().then_inc(s_tbl, 1)
            table(vec.tensor_tensor(shift, last, nblk, ALU.subtract))
            table(vec.scalar_tensor_tensor(shift, shift, float(P), ebase[:], ALU.mult, ALU.subtract))
            table(vec.tensor_tensor(own[0], eota[:].unsqueeze(1).broadcast_to([P, NT * K, E]),
                                    flat_k[0].unsqueeze(2).broadcast_to([P, NT * K, E]), ALU.is_equal))
            table(vec.tensor_tensor(own[1], own[0], shift.unsqueeze(1).broadcast_to([P, NT * K, E]), ALU.mult))
            table(vec.tensor_reduce(flat_k[0], own[1], AX.X, ALU.add))
            vec.tensor_tensor(flat_k[2], flat_k[1], flat_k[0], ALU.add).then_inc(s_place_out, 1)

            def step(at):
                if rows := at(1):
                    c, par, _, _ = rows
                    vec.wait_ge(s_bxhi[par], c)
                    vec.tensor_tensor(bxlo[par][:].rearrange("p k t -> p (k t)"), bank_x[par][:, 0:C],
                                      bxhi[par][:].rearrange("p k t -> p (k t)").bitcast(F32),
                                      ALU.subtract).then_inc(s_bx[par], 1)
                if now := at(0):
                    c, par, _, _ = now
                    vec.wait_ge(s_bsg[par], c)
                    vec.tensor_tensor(bprod[par][:, 0:H], bank_h[par][:, 0:H], bsg[par], ALU.mult)
                    vec.tensor_tensor(bprod[par][:, H:2 * P], bank_h[par][:, P:H], bsg[par][:, P:H],
                                      ALU.mult).then_inc(s_bpr[par], 1)
                if hidden := at(-1):
                    c, par, _, _ = hidden
                    vec.wait_ge(s_bhhi[par], c)
                    vec.tensor_tensor(bhlo[par][:], bank_t[par][:, 0:P], bhhi[par][:, 0, :].bitcast(F32), ALU.subtract)
                    vec.tensor_tensor(bhhi[par][HR:P, 1, :], bank_t[par][HR:P, P:2 * P],
                                      bhhi[par][HR:P, 1, :].bitcast(F32), ALU.subtract).then_inc(s_bht[par], 1)

            blocks(vec, step)

            def final(n, par):
                tile = (n - 1) * G if isinstance(n, int) else vec.snap((n - 1) * G)
                vec.wait_ge(s_got[par], (n + 1 - par) * (16 * K * G // 2))
                z = got[0][par]
                for t in range(G):
                    ins = vec.scalar_tensor_tensor(z[:, t:t + 1, :], z[:, t:t + 1, :], topf[:, sl((tile + t) * K)],
                                                   xs[:, sl(tile + t), :], ALU.mult, ALU.add)
                ins.then_inc(s_first, 1)
                vec.wait_ge(s_first, n)
                for t in range(G):
                    ins = vec.scalar_tensor_tensor(z[:, t:t + 1, :], got[1][par][:, t:t + 1, :],
                                                   topf[:, sl((tile + t) * K + 1)], z[:, t:t + 1, :], ALU.mult, ALU.add)
                ins.then_inc(s_sum, 1)
                vec.wait_ge(s_sum, n)
                for t in range(G):
                    ins = vec.bn_stats(bst[:, t, :], z[:, t, :])
                ins.then_inc(s_bst, 1)
                vec.wait_ge(s_bst, n)
                vec.sem_inc(s_tick, 1)
                for t in range(G):
                    ins = vec.bn_aggr(fmv[:, t, :], bst[:, t, :])
                ins.then_inc(s_var, 1)
                vec.wait_ge(s_std, n)
                vec.reciprocal(frn[:, 1, :], frn[:, 0, :]).then_inc(s_n[0], 1)
                vec.wait_ge(s_n[0], n)
                vec.tensor_tensor(frn[:, 2, :], frn[:, 1, :], frn[:, 1, :], ALU.mult).then_inc(s_n[1], 1)
                vec.wait_ge(s_n[1], n)
                vec.scalar_tensor_tensor(frn[:, 2, :], fmv[:, :, 1], EPS, frn[:, 2, :], ALU.add, ALU.mult).then_inc(s_n[2], 1)
                vec.wait_ge(s_n[2], n)
                vec.tensor_scalar(frn[:, 2, :], frn[:, 2, :], -0.5, 1.5, ALU.mult, ALU.add).then_inc(s_n[3], 1)
                vec.wait_ge(s_n[3], n)
                vec.tensor_tensor(frn[:, 3, :], frn[:, 1, :], frn[:, 2, :], ALU.mult).then_inc(s_n[4], 1)
                vec.wait_ge(s_n[4], n)
                for t in range(G):
                    ins = vec.tensor_scalar(z[:, t, :], z[:, t, :], fmv[:, t, 0:1], frn[:, 3, t:t + 1], ALU.subtract,
                                            ALU.mult)
                ins.then_inc(s_fin, 1)

            groups(vec, final)


def kernel(**inputs):
    import concourse.bacc as bacc
    from concourse.bass_utils import run_bass_kernel_spmd

    def laid(a, *axes):
        return np.ascontiguousarray(np.transpose(inputs[a], axes) if axes else inputs[a])

    nc = bacc.Bacc("TRN2", target_bir_lowering=False, num_devices=1)
    arrays = {
        "x": laid("L0_attn_x"),
        "w_qkv": laid("L0_attn_w_qkv"),
        "w_kv_t": np.ascontiguousarray(np.transpose(inputs["L0_attn_w_qkv"])[:, C:]),
        "w_conv": np.ascontiguousarray(np.reshape(inputs["L0_attn_w_conv1"], (KC, P)).T),
        "gate_t": laid("L0_ffn_gate_w", 1, 0),
        "w1_t": laid("L0_ffn_W1", 0, 2, 1),
        "w2_t": laid("L0_ffn_W2", 0, 2, 1),
        "ws1_t": laid("L0_ffn_Ws1", 1, 0),
        "ws2_t": laid("L0_ffn_Ws2", 1, 0),
    }
    args = [nc.dram_tensor(n, a.shape, mybir.dt.from_np(a.dtype), kind="ExternalInput").ap() for n, a in arrays.items()]
    out = nc.dram_tensor("out", (B, N, C), F32, kind="ExternalOutput").ap()
    post_norm_layer(nc, *args, out)
    r = run_bass_kernel_spmd(nc, [arrays], core_ids=[0])
    return r.results[0]["out"]
```

```python
from contextlib import ExitStack

import numpy as np
import concourse.bass as bass
import concourse.mybir as mybir

F32 = mybir.dt.float32
F32R = mybir.dt.float32r
I32 = mybir.dt.int32
ALU = mybir.AluOpType
ACT = mybir.ActivationFunctionType
AX = mybir.AxisListType
RMAX = bass.bass_isa.ReduceOp.max
RADD = bass.bass_isa.ReduceOp.add

P = 128
B, N, C = 2, 2048, 256
TB = N // P
NT = B * TB
KC = C // P
E, K, H = 8, 2, 192
F = 2 * H
HS = 384
MC = HS // P
G = 4
GT = G * P
NG = NT // G
NP = NG // 2
EPS = 1e-5
SCALE = float(C) ** -0.5
CAP = B * N + P
BLOCKS = (K * B * N + E * (P - 1)) // P
NBK = -(-BLOCKS // 4) * 4
AHEAD = 3
IDLE = NBK - K * B * N // P
ROWS = E * CAP + IDLE * P
CX = C + 2
DUMMY = K * B * N
OUTS = DUMMY + NBK * P
LEAD = 4
UNITS = [(0, 2), (2, 2), (4, 2), (6, 1), (7, 1)]
HR = H - P


def post_norm_layer(nc, x, w_qkv, w_kv_t, w_conv, gate_t, w1_t, w2_t, ws1_t, ws2_t, out):
    rows_in = nc.dram_tensor("rows_in", [ROWS, CX], F32, kind="Internal").ap()
    rows_out = nc.dram_tensor("rows_out", [OUTS, C], F32, kind="Internal").ap()

    with ExitStack() as ctx:
        def sb(name, shape, dt=F32):
            return ctx.enter_context(nc.sbuf_tensor(name, shape, dt))

        def sem(name):
            return ctx.enter_context(nc.semaphore(name))

        def pair(name):
            return [sem(f"{name}_even"), sem(f"{name}_odd")]

        xs = sb("xs", [P, NT, C])
        w1hi, w1lo = (sb(f"w1{n}", [P, E, KC, F], F32R) for n in ("hi", "lo"))
        w2hi, w2lo = (sb(f"w2{n}", [P, E, C], F32R) for n in ("hi", "lo"))
        w2rhi, w2rlo = (sb(f"w2r{n}", [P, E, C], F32R) for n in ("hi", "lo"))
        ws1hi, ws1lo = (sb(f"ws1{n}", [P, KC, 2 * HS], F32R) for n in ("hi", "lo"))
        ws2hi, ws2lo = (sb(f"ws2{n}", [P, MC, C], F32R) for n in ("hi", "lo"))
        x2 = [sb(f"x2_{n}", [P, G, CX]) for n in range(2)]
        xthi, xtlo = (sb(f"xt{n}", [P, KC, GT], F32R) for n in ("hi", "lo"))
        hthi, htlo = (sb(f"ht{n}", [P, MC, GT], F32R) for n in ("hi", "lo"))
        mix = sb("mix", [P, 4, GT])
        stage = sb("stage", [P, 2, 3072])
        bxhi, bxlo = ([sb(f"bx{n}{i}", [P, KC, P], F32R) for i in range(2)] for n in ("hi", "lo"))
        bhhi = [sb(f"bhhi{i}", [P, 2, P], F32R) for i in range(2)]
        bhlo = [sb(f"bhlo{i}", [P, P], F32R) for i in range(2)]
        ones = sb("ones", [P, P])
        ident = sb("ident", [P, P])
        tri = sb("tri", [P, P])
        gatef = sb("gatef", [P, KC, E])
        gate = sb("gate", [P, KC, 2, E], F32R)
        wcol = sb("wcol", [P, KC])
        epst = sb("epst", [P, 1])
        agent = sb("agent", [P, B, TB])
        tok = sb("tok", [P, B, TB])
        tok2 = sb("tok2", [P, B, TB])
        lv = sb("lv", [P, B, TB])
        att = sb("att", [P, C])
        small = sb("small", [P, B, 8])
        bst = sb("bst", [P, G, 6])
        mv = sb("mv", [P, NT, 2])
        rstd = sb("rstd", [P, NT])
        rn = sb("rn", [P, 3, TB])
        top = sb("top", [P, NT, K])
        slot = sb("slot", [P, NT, K], I32)
        twice = sb("twice", [P, NT])
        row = sb("row", [P, 4])
        spare = sb("spare", [P, NBK])
        place = sb("place", [P, NBK], I32)
        rt = sb("rt", [P, 9, G, E])
        r4 = sb("r4", [P, 3, G])
        seen = sb("seen", [P, E])
        ebase = sb("ebase", [P, E])
        jota = sb("jota", [P, NBK])
        thr = sb("thr", [P, NT])
        te = sb("te", [P, 2, NBK])
        tc = sb("tc", [P, 6, E])
        clear = sb("clear", [P, CX])
        m8 = sb("m8", [P, G, 8])
        i8 = sb("i8", [P, G, 8], mybir.dt.uint32)
        eota = sb("eota", [P, E])
        zrow = sb("zrow", [1, E], I32)
        brow = sb("brow", [1, NBK], I32)
        bexp = sb("bexp", [1, NBK], I32)
        bexpf = sb("bexpf", [P, NBK])
        pack = sb("pack", [1, NBK // 4 - 1])
        packed = sb("packed", [1, NBK // 4 - 1], I32)
        banks = [ctx.enter_context(nc.psum_tensor(f"bank{n}", [P, 512], F32)) for n in range(8)]

        wq = mix[:, 0, :].rearrange("p (k c) -> p k c", k=KC)
        sum_row = mix[:, 0, :]
        wv = mix[:, 1, :].rearrange("p (k c) -> p k c", k=KC)
        wkvt = mix[:, 2:4, :]
        sg = [mix[:, n, :] for n in range(2)]
        prod = [mix[:, 2 + n, :] for n in range(2)]
        wide = x2[0][:, :, 0:C]
        junk = x2[1][:, :, 0:C]
        flat = stage[:, 0, :]
        xg = [flat[:, n * CX:(n + 1) * CX] for n in range(4)]
        at_sg = 4 * CX + 8
        at_prod = at_sg + 2 * H
        at_y = at_prod + 2 * 2 * P
        bsg = [flat[:, at_sg + n * H:at_sg + (n + 1) * H] for n in range(2)]
        bprod = [flat[:, at_prod + n * 2 * P:at_prod + (n + 1) * 2 * P] for n in range(2)]
        by = [flat[:, at_y + n * C:at_y + (n + 1) * C] for n in range(4)]
        room = [stage[:, n, 0:G * K * C] for n in range(2)]
        for w in (w1hi, w1lo):
            w1f = w[:].bitcast(F32).rearrange("p e k f -> p (e k f)")
            room += [w1f[:, n * G * K * C:(n + 1) * G * K * C] for n in range(3)]
        got = [a.rearrange("p (t k c) -> p t k c", t=G, k=K) for a in room]
        ln2 = [rt[:, n].rearrange("p t e -> p (t e)") for n in range(5)]
        mvf = mv[:].rearrange("p t s -> p (t s)")
        tokf = tok[:].rearrange("p b t -> p (b t)")
        agentf = agent[:].rearrange("p b t -> p (b t)")
        lvf = lv[:].rearrange("p b t -> p (b t)")

        bank_x, bank_y, bank_h, bank_t = banks[0:2], banks[2:4], banks[4:6], banks[6:8]

        s_x = [sem(f"x_loaded{n}") for n in range(2 * B)]
        s_wq, s_wkv, s_gate = sem("wq_loaded"), sem("wkv_loaded"), sem("gate_loaded")
        s_raw = [sem(f"raw_loaded{n}") for n in range(5)]
        s_whi, s_wlo, s_gset = sem("weights_hi"), sem("weights_lo"), sem("gate_split")
        s_mem, s_set = sem("cleared"), sem("constants")
        s_pad = sem("padding_written")
        s_dve, s_pe, s_act, s_pool = sem("att_vector"), sem("att_tensor"), sem("att_scalar"), sem("att_pool")
        s_ag, s_lv = sem("agent"), sem("token_logits")
        s_add, s_stat, s_agg = sem("att_added"), sem("ln1_sums"), sem("ln1_stats")

        s_x2, s_xtp, s_xhi, s_xt = sem("x2"), sem("x2t_psum"), sem("x2t_hi"), sem("x2t")
        s_lg, s_sh, s_ex, s_m = sem("logits"), sem("logits_shifted"), sem("exps"), sem("chosen")
        s_pos, s_slot, s_sc = sem("positions"), sem("slots"), pair("scattered")
        (s_lsum, s_lmax, s_esum, s_rcp, s_score, s_top8, s_idx, s_sel, s_place, s_tmp) = (
            sem(f"route_{n}") for n in ("logits", "max", "sum", "reciprocal", "scores", "top8", "index", "masks",
                                        "places", "terms"))
        s_h = [sem(f"hidden_psum{m}") for m in range(MC)]
        s_sg = [sem(f"silu{m}") for m in range(MC)]
        s_pr = [sem(f"product{m}") for m in range(MC)]
        s_hhi = [sem(f"hidden_hi{m}") for m in range(MC)]
        s_ht = sem("hidden")
        s_z = [sem(f"shared_psum{u}") for u in range(2)]
        s_zev = [sem(f"shared_added{u}") for u in range(2)]
        s_cnt, s_tb, s_tbl, s_pack = (sem("counts"), sem("table_steps"), sem("block_table"),
                                       sem("experts_packed"))
        s_ends = sem("ends_of_regions")
        s_row, s_to = sem("block_rows"), sem("block_places")

        s_ld = [sem(f"rows_loaded{n}") for n in range(4)]
        s_bxp, s_bxhi, s_bx = pair("rows_t_psum"), pair("rows_t_hi"), pair("rows_t")
        s_bh, s_bsg, s_bpr = pair("expert_hidden"), pair("expert_silu"), pair("expert_product")
        s_bhp, s_bhhi, s_bht = pair("expert_ht_psum"), pair("expert_ht_hi"), pair("expert_ht")
        s_by, s_byev = pair("expert_out"), pair("expert_row")
        s_st = [sem(f"rows_stored{n}") for n in range(4)]

        s_got = [sem(f"results_loaded{q}") for q in range(NG)]
        s_weighed, s_first, s_sum = sem("first_weighed"), sem("first_added"), sem("summed")
        s_bst, s_var, s_std = sem("ln2_sums"), sem("ln2_stats"), sem("ln2_std")
        s_n = [sem(f"ln2_newton{n}") for n in range(5)]
        s_shift = sem("ln2_shift")
        s_fin, s_out, s_tick = sem("ln2_ready"), sem("out_stored"), sem("wait_taken")
        s_tock = sem("load_wait_taken")

        block = ctx.enter_context(nc.Block())

        NEWTON = ("std_rcp", "square", "times_var", "newton", "rstd")
        DVE = ["tok_shift0", "g_row0", "g0", "tok_shift1", "max0", "tok_rcp0", "tok_rcp1", "tok0", "tok1", "sum_rcp0",
               "att0", "col0", "lmax0", "lneg0", "psum_rcp0", "g_row1", "g1", "max1", "sum_rcp1", "att1", "col1",
               "lmax1", "lneg1", "psum_rcp1",
               "s_row0", "s0", *(n + "0" for n in NEWTON), "s_row1", "s1", *(n + "1" for n in NEWTON)]
        PE = ["g0", "g_spread0", "logits0", "col0", "r0", "g1", "g_spread1", "logits1", "col1", "r1", "s0", "s_spread0", "value0",
              "s1", "s_spread1", "value1"]
        SCALAR = ["tok_exp0", "tok_exp1", "exp0", "p0", "exp1", "p1", "std0", "value1", "std1"]
        POOL = ["max0", "sum0", "max1", "sum1"]

        def dve(b, name):
            return 2 + DVE.index(f"{name}{b}")

        def pe_at(b, name):
            return 2 + PE.index(f"{name}{b}")

        def act_at(b, name):
            return 1 + SCALAR.index(f"{name}{b}")

        def pool_at(b, name):
            return 1 + POOL.index(f"{name}{b}")

        def sl(start, size=1):
            return slice(start, start + size) if isinstance(start, int) else bass.ds(start, size)

        def groups(eng, body):
            for n in (1, 2):
                body(n, (n - 1) % 2)
            with eng.Fori(2, NP) as i:
                body(eng.snap(2 * i - 1), 0)
                body(eng.snap(2 * i), 1)
            for n in (NG - 1, NG):
                body(n, (n - 1) % 2)

        def later(n, by=1):
            return not isinstance(n, int) or n > by

        def more(n):
            return not isinstance(n, int) or n < NG

        def nth(n, of, k):
            return (n - 1) * of + k + 1

        def blocks(eng, step, each_four=None):
            def static(j):
                def at(d):
                    b = j + d
                    return (b // 2 + 1, b % 2, b // 4 + 1, b % 4) if 0 <= b < NBK else None
                return at
            for j in range(-AHEAD, 8):
                if each_four and j == 4:
                    each_four(j // 4)
                step(static(j))
            with eng.Fori(2, NBK // 4 - 1) as i:
                known = {}
                if each_four:
                    each_four(i)

                def count(times, off):
                    if (times, off) not in known:
                        known[times, off] = eng.snap(times * i + off)
                    return known[times, off]

                for o in range(4):
                    step(lambda d, o=o: (count(2, (o + d) // 2 + 1), (o + d) % 2, count(1, (o + d) // 4 + 1), (o + d) % 4))
            for j in range(NBK - 4, NBK + 2):
                if each_four and j % 4 == 0:
                    each_four(j // 4 if j < NBK else None)
                step(static(j))

        def block_id(c, par):
            return sl((c - 1) * 2 + par)

        def pad_regions(eng, experts):
            eng.wait_ge(s_mem, 2)
            eng.wait_ge(s_ends, 1)
            for e in experts:
                r = eng.value_load(zrow[0:1, e:e + 1], min_val=0, max_val=ROWS - P)
                eng.dma_start(rows_in[bass.ds(r, P), :], clear[:]).then_inc(s_pad, 16)

        S1 = KC * 2 * HS
        RAW = [stage[:, 0, 0:S1 + MC * C], stage[:, 1, 0:4 * KC * F], stage[:, 0, 0:4 * KC * F],
               stage[:, 1, 0:E * C], stage[:, 0, 0:E * C]]

        def parts(s1, s2, a, b, r):
            return [[(s1[:].rearrange("p k f -> p (k f)"), RAW[0][:, 0:S1]),
                     (s2[:].rearrange("p m c -> p (m c)"), RAW[0][:, S1:])],
                    [(a[:, 0:4].rearrange("p e k f -> p (e k f)"), RAW[1])],
                    [(a[:, 4:8].rearrange("p e k f -> p (e k f)"), RAW[2])],
                    [(b[:].rearrange("p e c -> p (e c)"), RAW[3])],
                    [(r[:].rearrange("p e c -> p (e c)"), RAW[4])]]

        HI = parts(ws1hi, ws2hi, w1hi, w2hi, w2rhi)
        LO = parts(ws1lo, ws2lo, w1lo, w2lo, w2rlo)
        SPLIT = [2, 3, 4, 5, 6]

        @block.sync
        def _(sp):
            sp.dma_start(wq, w_qkv[0:C].rearrange("(k p) c -> p k c", p=P)).then_inc(s_wq, 16)
            sp.dma_start(wcol[:], w_conv).then_inc(s_wq, 16)
            for n in range(2 * B):
                half = slice(n % 2 * TB // 2, (n % 2 + 1) * TB // 2)
                sp.dma_start(xs[:, n * TB // 2:(n + 1) * TB // 2, :],
                             x[n // 2].rearrange("(p j) c -> p j c", j=TB)[:, half, :]).then_inc(s_x[n], 16)
            sp.dma_start(wkvt, w_kv_t.rearrange("(k p) c -> p k c", p=P)).then_inc(s_wkv, 16)
            sp.dma_start(wv, w_qkv[2 * C:3 * C].rearrange("(k p) c -> p k c", p=P)).then_inc(s_wkv, 16)
            sp.dma_start(gatef[:], gate_t.rearrange("(k p) e -> p k e", p=P)).then_inc(s_gate, 16)
            sp.dma_start(RAW[0][:, 0:S1].rearrange("p (k f) -> p k f", k=KC),
                         ws1_t.rearrange("(k p) f -> p k f", p=P)).then_inc(s_raw[0], 16)
            sp.dma_start(RAW[0][:, S1:].rearrange("p (m c) -> p m c", m=MC),
                         ws2_t.rearrange("(m p) c -> p m c", p=P)).then_inc(s_raw[0], 16)
            for n in range(2):
                if n == 1:
                    sp.wait_ge(s_whi, SPLIT[0])
                    sp.wait_ge(s_wlo, SPLIT[0])
                for e in range(4):
                    sp.dma_start(RAW[1 + n].rearrange("p (e k f) -> p e k f", e=4, k=KC)[:, e],
                                 w1_t[4 * n + e].rearrange("(k p) f -> p k f", p=P)).then_inc(s_raw[1 + n], 16)
            sp.wait_ge(s_whi, SPLIT[1])
            sp.wait_ge(s_wlo, SPLIT[1])
            sp.dma_start(RAW[3].rearrange("p (e c) -> p e c", e=E),
                         w2_t[:, 0:P].rearrange("e p c -> p e c")).then_inc(s_raw[3], 16)
            sp.wait_ge(s_whi, SPLIT[2])
            sp.wait_ge(s_wlo, SPLIT[2])
            for n in range(2):
                sp.dma_start(RAW[4][n * HR:(n + 1) * HR].rearrange("p (e c) -> p e c", e=E),
                             w2_t[:, P:H].rearrange("e p c -> p e c")).then_inc(s_raw[4], 16)
            sp.wait_ge(s_mem, 2)
            for n in range(IDLE):
                sp.dma_start(rows_in[E * CAP + n * P:E * CAP + (n + 1) * P, :], clear[:]).then_inc(s_pad, 16)
            pad_regions(sp, range(0, E // 2))
            for n in range(2):
                sp.wait_ge(s_sc[n], 16 * K * G * NP)
            sp.wait_ge(s_pad, 16 * (IDLE + E))
            sp.wait_ge(s_tbl, 1)
            sp.wait_ge(s_whi, SPLIT[4])
            sp.wait_ge(s_wlo, SPLIT[4])

            def step(at):
                if load := at(AHEAD):
                    c, par, quad, buf = load
                    if not (isinstance(quad, int) and quad == 1):
                        sp.wait_ge(s_to, (quad - 2) * 4 + buf + 1)
                        sp.sem_inc(s_tock, 1)
                    if not (isinstance(c, int) and c <= 2):
                        sp.wait_ge(s_bxp[par], c - 2)
                        sp.sem_inc(s_tock, 1)
                    r = sp.value_load(brow[0:1, block_id(c, par)], min_val=0, max_val=ROWS - P)
                    sp.dma_start(xg[buf], rows_in[bass.ds(r, P), :]).then_inc(s_ld[buf], 16)

            blocks(sp, step)
            for n in range(4):
                sp.wait_ge(s_st[n], 16 * (NBK // 4))
            tokens = rows_out[0:DUMMY].rearrange("(b p j k) c -> b p j k c", b=B, p=P, k=K)
            for q in range(NG):
                sp.dma_start(got[q], tokens[q * G // TB][:, q * G % TB:q * G % TB + G]).then_inc(s_got[q], 16)
            for q in range(NG):
                sp.wait_ge(s_fin, q + 1)
                sp.dma_start(out[q * G // TB].rearrange("(p j) c -> p j c", j=TB)[:, q * G % TB:q * G % TB + G, :],
                             xs[:, q * G:(q + 1) * G, :]).then_inc(s_out, 16)
            sp.wait_ge(s_out, 16 * NG)

        @block.gpsimd
        def _(pool):
            pool.memset(ones[:], 1.0).then_inc(s_mem, 1)
            pool.memset(ident[:], 0.0)
            pool.memset(epst[:], EPS)
            pool.memset(seen[:], 0.0)
            pool.memset(tri[:], 1.0)
            pool.memset(clear[:, 0:C], 0.0)
            pool.memset(clear[:, C:CX], float(OUTS)).then_inc(s_mem, 1)
            pool.wait_ge(s_mem, 2)
            pool.affine_select(out=ident[:], in_=ident[:], compare_op=ALU.not_equal, fill=1.0, base=0,
                               pattern=[[-1, P]], channel_multiplier=1)
            pool.affine_select(out=tri[:], in_=tri[:], compare_op=ALU.is_gt, fill=0.0, base=0,
                               pattern=[[1, P]], channel_multiplier=-1)
            pool.iota(ebase[:], [[CAP, E]], base=0, channel_multiplier=0, allow_small_or_imprecise_dtypes=True)
            pool.iota(eota[:], [[1, E]], base=0, channel_multiplier=0, allow_small_or_imprecise_dtypes=True)
            pool.iota(jota[:], [[1, NBK]], base=0, channel_multiplier=0, allow_small_or_imprecise_dtypes=True)
            pool.iota(twice[:], [[K * N, B], [K, TB]], base=0, channel_multiplier=K * TB,
                      allow_small_or_imprecise_dtypes=True)
            pool.iota(spare[:], [[P, NBK]], base=DUMMY, channel_multiplier=1, allow_small_or_imprecise_dtypes=True)
            pool.iota(thr[:], [[P, NT]], base=0, channel_multiplier=0,
                      allow_small_or_imprecise_dtypes=True).then_inc(s_set, 1)

            def low(n):
                for m, (dst, src) in enumerate(LO[n]):
                    pool.wait_ge(s_whi, SPLIT[n])
                    pool.tensor_tensor(dst, src, HI[n][m][0].bitcast(F32), ALU.subtract).then_inc(s_wlo, 1)

            low(0)
            for b in range(B):
                pool.wait_ge(s_dve, dve(b, "lmax"))
                pool.partition_all_reduce(small[:, b, 3:4], small[:, b, 2:3], P, RMAX).then_inc(s_pool, 1)
                pool.wait_ge(s_act, act_at(b, "p"))
                pool.partition_all_reduce(small[:, b, 6:7], small[:, b, 5:6], P, RADD).then_inc(s_pool, 1)
                for n in (1 + 2 * b, 2 + 2 * b):
                    low(n)
            for q in range(NG):
                pool.wait_ge(s_slot, q + 1)
                for t in range(G):
                    for k in range(K):
                        pool.indirect_dma_start(
                            rows_in[0:E * CAP, :], bass.IndirectOffsetOnAxis(slot[:, q * G + t, k:k + 1], 0),
                            x2[q % 2][:, t, :], None).then_inc(s_sc[q % 2], 16)
            pool.wait_ge(s_tbl, 1)
            for j in range(-LEAD, NBK):
                ahead = j + LEAD
                if ahead < NBK:
                    buf = ahead % 4
                    pool.wait_ge(s_ld[buf], 16 * (ahead // 4 + 1))
                    pool.tensor_scalar(row[:, buf:buf + 1], xg[buf][:, C + 1:CX], bexpf[:, ahead:ahead + 1],
                                       xg[buf][:, C:C + 1], ALU.is_equal, ALU.add).then_inc(s_row, 1)
                    pool.wait_ge(s_row, ahead + 1)
                    pool.tensor_scalar(place[:, ahead:ahead + 1], row[:, buf:buf + 1], spare[:, ahead:ahead + 1], None,
                                       ALU.min).then_inc(s_to, 1)
                if j >= 0:
                    pool.wait_ge(s_to, j + 1)
                    pool.wait_ge(s_byev[j % 2], j // 2 + 1)
                    pool.indirect_dma_start(rows_out[:, :], bass.IndirectOffsetOnAxis(place[:, j:j + 1], 0), by[j % 4],
                                            None).then_inc(s_st[j % 4], 16)

            for q in range(NG):
                pool.wait_ge(s_weighed, q + 1)
                rows = xs[:, q * G:(q + 1) * G, :]
                pool.tensor_tensor(rows, got[q][:, :, 0, :], rows, ALU.add).then_inc(s_first, 1)

        @block.scalar
        def _(act):
            def high(n, dmas):
                act.wait_ge(s_raw[n], 16 * dmas)
                for dst, src in HI[n]:
                    act.activation(dst, src, ACT.Copy).then_inc(s_whi, 1)

            def channel_exp(b):
                act.wait_ge(s_dve, dve(b, "max"))
                if b:
                    act.wait_ge(s_pe, pe_at(b - 1, "col"))
                act.activation(att[:], banks[2][:, b * C:(b + 1) * C], ACT.Exp, bias=small[:, b, 0:1],
                               accum_out=small[:, b, 1:2]).then_inc(s_act, 1)

            def token_exp(b):
                act.wait_ge(s_dve, dve(b, "lneg"))
                act.activation(lv[:, b, :], lv[:, b, :], ACT.Exp, bias=small[:, b, 4:5],
                               accum_out=small[:, b, 5:6]).then_inc(s_act, 1)

            def std(b):
                act.wait_ge(s_agg, NP * (b + 1))
                act.activation(rn[:, 0, :], mv[:, b * TB:(b + 1) * TB, 1], ACT.Sqrt, bias=epst[:]).then_inc(s_act, 1)

            for b in range(B):
                act.wait_ge(s_dve, dve(b, "tok_shift"))
                act.activation(tok[:, b, :], tok2[:, b, :], ACT.Exp).then_inc(s_act, 1)
            channel_exp(0)
            high(0, 2)
            high(1, 4)
            token_exp(0)
            channel_exp(1)
            high(2, 4)
            high(3, 1)
            token_exp(1)
            high(4, 2)
            std(0)

            def rows_hi(n):
                if later(n):
                    act.wait_ge(s_h[MC - 1], n - 1)
                for k in range(KC):
                    act.wait_ge(s_xtp, nth(n, KC, k))
                    act.activation(xthi[:, k, :], banks[k][:], ACT.Copy).then_inc(s_xhi, 1)

            def group(n, par):
                act.wait_ge(s_sh, n)
                act.activation(rt[:, 2], rt[:, 1], ACT.Exp).then_inc(s_ex, 1)
                act.preload_act_table(ACT.Silu)
                for m in range(MC):
                    buf = (par + m) % 2
                    act.wait_ge(s_h[m], n)
                    act.activation(sg[buf], banks[5 + 2 * buf][:], ACT.Silu).then_inc(s_sg[m], 1)
                    if m == 0 and later(n):
                        act.wait_ge(s_z[1], n - 1)
                    act.wait_ge(s_pr[m], n)
                    act.activation(hthi[:, m, :], prod[buf], ACT.Copy).then_inc(s_hhi[m], 1)
                if more(n):
                    rows_hi(n + 1)
                    if isinstance(n, int) and n == 2:
                        std(1)
                    act.preload_act_table(ACT.Exp)

            rows_hi(1)
            act.preload_act_table(ACT.Exp)
            act.wait_ge(s_pe, pe_at(1, "value"))
            act.activation(att[:], banks[3][:, C:2 * C], ACT.Copy).then_inc(s_act, 1)
            groups(act, group)
            pad_regions(act, range(E // 2, E))
            act.preload_act_table(ACT.Silu)

            def step(at):
                if rows := at(1):
                    c, par, _, _ = rows
                    act.wait_ge(s_bxp[par], c)
                    act.activation(bxhi[par][:].rearrange("p k t -> p (k t)"), bank_x[par][:, 0:C],
                                   ACT.Copy).then_inc(s_bxhi[par], 1)
                if now := at(0):
                    c, par, _, _ = now
                    act.wait_ge(s_bh[par], c)
                    act.activation(bsg[par], bank_h[par][:, H:F], ACT.Silu).then_inc(s_bsg[par], 1)
                if hidden := at(-1):
                    c, par, _, _ = hidden
                    act.wait_ge(s_bhp[par], c)
                    act.activation(bhhi[par][:].rearrange("p k t -> p (k t)"), bank_t[par][:, 0:2 * P],
                                   ACT.Copy).then_inc(s_bhhi[par], 1)
                if result := at(-2):
                    c, par, quad, buf = result
                    act.wait_ge(s_by[par], c)
                    if not (isinstance(quad, int) and quad == 1):
                        act.wait_ge(s_st[buf], 16 * (quad - 1))
                    act.activation(by[buf], bank_y[par][:, 0:C], ACT.Copy).then_inc(s_byev[par], 1)

            blocks(act, step)
            act.preload_act_table(ACT.Sqrt)

            def weigh_first(q):
                act.wait_ge(s_got[q], 16)
                for t in range(G):
                    first = got[q][:, t, 0, :]
                    ins = act.activation(first, first, ACT.Copy, scale=top[:, q * G + t, 0:1])
                ins.then_inc(s_weighed, 1)

            for q in range(3):
                weigh_first(q)
            std = ln2[0]
            for u, (start, size) in enumerate(UNITS):
                tiles = slice(start * G, (start + size) * G)
                act.wait_ge(s_var, start + size)
                act.activation(std[:, tiles], mv[:, tiles, 1], ACT.Sqrt, bias=epst[:]).then_inc(s_std, 1)
                for q in range(start + 3, min(start + 3 + size, NG)):
                    weigh_first(q)
                act.wait_ge(s_shift, u + 1)
                for q in range(start, start + size):
                    for t in range(q * G, (q + 1) * G):
                        ins = act.activation(xs[:, t, :], xs[:, t, :], ACT.Identity, bias=ln2[4][:, t:t + 1],
                                             scale=ln2[3][:, t:t + 1])
                    ins.then_inc(s_fin, 1)

        @block.tensor
        def _(pe):
            pe.wait_ge(s_wq, 32)
            pe.wait_ge(s_dve, 1)
            for k in range(KC):
                mm = pe.matmul(banks[0][:, 0:C], wide[:, 0, k * P:(k + 1) * P], wq[:, k, :],
                               start=(k == 0), stop=(k == KC - 1))
            mm.then_inc(s_pe, 1)

            def weighted_sum(row, b, weight, ready=None):
                for t in range(TB):
                    if ready:
                        pe.wait_ge(ready, b * TB + t + 1)
                    mm = pe.matmul(row[0:1, b * C:(b + 1) * C], weight[:, b, t:t + 1], xs[:, b * TB + t, :],
                                   start=(t == 0), stop=(t == TB - 1))
                return mm

            def row_to_columns(b):
                for k in range(KC):
                    part = slice(b * C + k * P, b * C + (k + 1) * P)
                    mm = pe.matmul(banks[7][:, part], sum_row[0:1, part], ones[0:1, :], start=True, stop=True)
                return mm

            def with_matrix(row, spread, matrix):
                for k in range(KC):
                    mm = pe.matmul(row, spread[:, k * P:(k + 1) * P], matrix(k), start=(k == 0), stop=(k == KC - 1))
                return mm

            def channel_sums(b):
                weighted_sum(banks[1], b, agent, s_ag).then_inc(s_pe, 1)
                pe.wait_ge(s_dve, dve(b, "g_row"))
                row_to_columns(b).then_inc(s_pe, 1)

            def channel_logits(b):
                pe.wait_ge(s_dve, dve(b, "g"))
                pe.wait_ge(s_wkv, 32)
                with_matrix(banks[2][:, b * C:(b + 1) * C], wide[:, 1 + b], lambda k: wkvt[:, k, 0:C]).then_inc(s_pe, 1)

            def column_and_r(b):
                pe.wait_ge(s_dve, dve(b, "att"))
                for k in range(KC):
                    mm = pe.matmul(banks[3][:, 8 * b + k:8 * b + k + 1], att[0:1, k * P:(k + 1) * P], ones[0:1, 0:1],
                                   start=True, stop=True)
                mm.then_inc(s_pe, 1)
                pe.wait_ge(s_dve, dve(b, "col"))
                with_matrix(banks[4][:, b * C:(b + 1) * C], wide[:, 1 + b], lambda k: wv[:, k, :]).then_inc(s_pe, 1)

            def token_sums(b):
                pe.wait_ge(s_act, act_at(b, "p"))
                weighted_sum(banks[5], b, lv).then_inc(s_pe, 1)

            def spread_token_sums(b):
                pe.wait_ge(s_dve, dve(b, "s_row"))
                row_to_columns(b).then_inc(s_pe, 1)

            def value(b, row, spread):
                pe.wait_ge(s_dve, dve(b, "s"))
                with_matrix(row, spread, lambda k: wkvt[:, k, C:2 * C]).then_inc(s_pe, 1)

            channel_sums(0)
            channel_logits(0)
            column_and_r(0)
            channel_sums(1)
            channel_logits(1)
            column_and_r(1)
            token_sums(0)
            spread_token_sums(0)
            value(0, banks[6][:, 0:C], wide[:, 1])
            token_sums(1)

            pe.wait_ge(s_set, 1)
            pe.wait_ge(s_gset, 2)
            pe.wait_ge(s_wlo, SPLIT[0])

            def transposes(n, par):
                pe.wait_ge(s_x2, n)
                for k in range(KC):
                    for t in range(G):
                        mm = pe.transpose(banks[k][:, t * P:(t + 1) * P], x2[par][:, t, k * P:(k + 1) * P], ident[:])
                    mm.then_inc(s_xtp, 1)

            def places(n):
                pe.wait_ge(s_m, n)
                chosen = rt[:, 7].rearrange("p t e -> p (t e)")
                pe.matmul(banks[2][:, 64:64 + G * E], tri[:], chosen, start=True, stop=False)
                for d in range(1, G):
                    pe.matmul(banks[2][:, 64 + d * E:64 + G * E], ones[:], chosen[:, 0:(G - d) * E],
                              start=False, stop=False)
                pe.matmul(banks[2][:, 64:64 + G * E].rearrange("p (t e) -> p t e", t=G), ones[:],
                          seen[:].unsqueeze(1).broadcast_to([P, G, E]), start=False, stop=True).then_inc(s_pos, 1)

            def group(n, par):
                if later(n):
                    pe.wait_ge(s_place, n - 1)
                pe.wait_ge(s_xt, n)
                for t in range(G):
                    steps = [(xt, k) for xt in (xthi, xtlo) for k in range(KC)]
                    for a, (xt, k) in enumerate(steps):
                        mm = pe.matmul(banks[2][:, t * 2 * E:(t + 1) * 2 * E], xt[:, k, t * P:(t + 1) * P],
                                       gate[:, k].rearrange("p h e -> p (h e)"),
                                       start=(a == 0), stop=(a == len(steps) - 1))
                mm.then_inc(s_lg, 1)
                for m in range(MC):
                    buf = (par + m) % 2
                    if m == 2:
                        pe.wait_ge(s_pr[0], n)
                    elif later(n):
                        pe.wait_ge(s_pr[m + 1], n - 1)
                        if m == 0:
                            pe.wait_ge(s_zev[0], n - 1)
                    for o, bank in ((m * P, banks[4 + 2 * buf]), (HS + m * P, banks[5 + 2 * buf])):
                        steps = [(w, xt, k) for w, xt in ((ws1hi, xthi), (ws1hi, xtlo), (ws1lo, xthi)) for k in range(KC)]
                        for a, (w, xt, k) in enumerate(steps):
                            mm = pe.matmul(bank[:], w[:, k, o:o + P], xt[:, k, :],
                                           start=(a == 0), stop=(a == len(steps) - 1))
                    mm.then_inc(s_h[m], 1)
                    if m == 1 and not more(n):
                        places(n)
                if not more(n):
                    pe.wait_ge(s_slot, NG)
                    pe.matmul(banks[2][:, 128:128 + E], ones[:], seen[:], start=True, stop=True).then_inc(s_cnt, 1)
                pe.wait_ge(s_pr[1], n)
                if later(n):
                    pe.wait_ge(s_zev[1], n - 1)

                def second_layer(t, chunks):
                    bank = (banks[4 + 2 * (1 - par)], banks[3])[t // 2]
                    for m in chunks:
                        steps = [(hthi, ws2hi), (htlo, ws2hi), (hthi, ws2lo)]
                        for a, (ht, w) in enumerate(steps):
                            mm = pe.matmul(bank[:, (t % 2) * C:(t % 2 + 1) * C], ht[:, m, t * P:(t + 1) * P],
                                           w[:, m, :], start=(m == 0 and a == 0), stop=(m == MC - 1 and a == len(steps) - 1))
                    return mm

                for m in range(MC - 1):
                    pe.wait_ge(s_ht, nth(n, MC, m))
                    second_layer(0, [m])
                second_layer(2, range(MC - 1))
                if more(n):
                    transposes(n + 1, 1 - par)
                    places(n)
                pe.wait_ge(s_ht, nth(n, MC, MC - 1))
                second_layer(0, [MC - 1])
                second_layer(1, range(MC)).then_inc(s_z[0], 1)
                second_layer(2, [MC - 1])
                second_layer(3, range(MC)).then_inc(s_z[1], 1)

            transposes(1, 0)
            spread_token_sums(1)
            value(1, banks[3][:, C:2 * C], junk[:, G - 1])
            groups(pe, group)
            pe.wait_ge(s_tbl, 1)
            pe.wait_ge(s_zev[1], NG)
            pe.wait_ge(s_wlo, SPLIT[4])

            four = []

            def load_experts(i):
                four.clear()
                if i is None:
                    return
                if isinstance(i, int) and i == 1:
                    pe.wait_ge(s_pack, 1)
                word = pe.value_load(packed[0:1, sl(i - 1)], min_val=0, max_val=E ** 6 - 1)
                four[:] = [pe.snap((word >> (3 * k)) & (E - 1)) for k in range(6)]

            def expert(c, par, k):
                return four[k] if four else pe.value_load(bexp[0:1, block_id(c, par)], min_val=0, max_val=E - 1)

            def step(at):
                if rows := at(1):
                    c, par, quad, buf = rows
                    pe.wait_ge(s_ld[buf], 16 * quad)
                    for k in range(KC):
                        mm = pe.transpose(bank_x[par][:, k * P:(k + 1) * P], xg[buf][:, k * P:(k + 1) * P], ident[:])
                    mm.then_inc(s_bxp[par], 1)
                if now := at(0):
                    c, par, _, buf = now
                    e = expert(c, par, buf + 2)
                    pe.wait_ge(s_bx[par], c)
                    steps = [(bx, w, k) for bx, w in ((bxhi, w1hi), (bxlo, w1hi), (bxhi, w1lo)) for k in range(KC)]
                    for a, (bx, w, k) in enumerate(steps):
                        mm = pe.matmul(bank_h[par][:, 0:F], bx[par][:, k, :], w[:, bass.ds(e, 1), k, :],
                                       start=(a == 0), stop=(a == len(steps) - 1))
                    mm.then_inc(s_bh[par], 1)
                if hidden := at(-1):
                    c, par, _, _ = hidden
                    pe.wait_ge(s_bpr[par], c)
                    for k in range(2):
                        mm = pe.transpose(bank_t[par][:, k * P:(k + 1) * P], bprod[par][:, k * P:(k + 1) * P], ident[:])
                    mm.then_inc(s_bhp[par], 1)
                if result := at(-2):
                    c, par, _, buf = result
                    e = expert(c, par, (buf + 2) % 4)
                    pe.wait_ge(s_bht[par], c)
                    if not (isinstance(c, int) and c == 1):
                        pe.wait_ge(s_byev[par], c - 1)
                    first, second = bhhi[par][:, 0, :], bhhi[par][:, 1, :]
                    steps = [(first, w2hi), (bhlo[par][:], w2hi), (first, w2lo), (second, w2rhi), (second, w2rlo)]
                    for a, (ht, w) in enumerate(steps):
                        mm = pe.matmul(bank_y[par][:, 0:C], ht, w[:, bass.ds(e, 1), :],
                                       start=(a == 0), stop=(a == len(steps) - 1))
                    mm.then_inc(s_by[par], 1)

            blocks(pe, step, load_experts)

        @block.vector
        def _(vec):
            def spread(dst, col, scale):
                for k in range(KC):
                    ins = vec.tensor_scalar(dst[:, k * P:(k + 1) * P], ones[:], col[:, k:k + 1], scale, ALU.mult, ALU.mult)
                return ins

            vec.wait_ge(s_wq, 32)
            vec.wait_ge(s_mem, 1)
            spread(wide[:, 0, :], wcol, 1.0).then_inc(s_dve, 1)
            def dots(row, dst, b, done, halves=(0, 1)):
                for t in range(b * TB + halves[0] * TB // 2, b * TB + (halves[-1] + 1) * TB // 2):
                    if t % (TB // 2) == 0:
                        vec.wait_ge(s_x[t // (TB // 2)], 16)
                    if t >= G:
                        vec.wait_ge(done, t - G + 1)
                    vec.tensor_tensor_reduce(junk[:, t % G, :], xs[:, t, :], row, 1.0, 0.0, ALU.mult, ALU.add,
                                             dst[:, t:t + 1]).then_inc(done, 1)

            def tok_shift(b):
                vec.wait_ge(s_ag, TB * (b + 1))
                vec.tensor_tensor(tok2[:, b, :], agent[:, b, :], agent[:, b, :], ALU.subtract).then_inc(s_dve, 1)

            def spread_sums(b):
                vec.wait_ge(s_pe, pe_at(b, "g"))
                vec.tensor_scalar(sum_row[0:1, b * C:(b + 1) * C], banks[1][0:1, b * C:(b + 1) * C], SCALE, None,
                                  ALU.mult).then_inc(s_dve, 1)
                vec.wait_ge(s_pe, pe_at(b, "g_spread"))
                vec.tensor_copy(wide[:, 1 + b, :], banks[7][:, b * C:(b + 1) * C]).then_inc(s_dve, 1)

            def channel_max(b):
                vec.wait_ge(s_pe, pe_at(b, "logits"))
                vec.tensor_reduce(small[:, b, 0:1], banks[2][:, b * C:(b + 1) * C], AX.X, ALU.max,
                                  negate=True).then_inc(s_dve, 1)

            def channel_softmax(b):
                vec.wait_ge(s_act, act_at(b, "exp"))
                vec.reciprocal(small[:, b, 7:8], small[:, b, 1:2]).then_inc(s_dve, 1)
                vec.wait_ge(s_dve, dve(b, "sum_rcp"))
                vec.tensor_scalar(att[0:1, :], att[0:1, :], small[0:1, b, 7:8], None, ALU.mult).then_inc(s_dve, 1)

            def spread_column(b):
                vec.wait_ge(s_pe, pe_at(b, "col"))
                spread(wide[:, 1 + b, :], banks[3][:, 8 * b:8 * b + KC], 1.0).then_inc(s_dve, 1)

            def token_logits(b):
                vec.wait_ge(s_pe, pe_at(b, "r"))
                dots(banks[4][:, b * C:(b + 1) * C], lvf, b, s_lv)
                vec.wait_ge(s_lv, TB * (b + 1))
                vec.tensor_reduce(small[:, b, 2:3], lv[:, b, :], AX.X, ALU.max).then_inc(s_dve, 1)
                vec.wait_ge(s_pool, pool_at(b, "max"))
                vec.tensor_scalar(small[:, b, 4:5], small[:, b, 3:4], -1.0, None, ALU.mult).then_inc(s_dve, 1)
                vec.wait_ge(s_pool, pool_at(b, "sum"))
                vec.reciprocal(small[:, b, 7:8], small[:, b, 6:7]).then_inc(s_dve, 1)

            def spread_value(b, dst):
                vec.wait_ge(s_pe, pe_at(b, "s"))
                vec.wait_ge(s_dve, dve(b, "psum_rcp"))
                vec.tensor_scalar(sum_row[0:1, b * C:(b + 1) * C], banks[5][0:1, b * C:(b + 1) * C], small[0:1, b, 7:8],
                                  None, ALU.mult).then_inc(s_dve, 1)
                vec.wait_ge(s_pe, pe_at(b, "s_spread"))
                vec.tensor_copy(dst, banks[7][:, b * C:(b + 1) * C]).then_inc(s_dve, 1)

            def add_attention(g, row):
                for t in range(g * G, (g + 1) * G):
                    ins = vec.scalar_tensor_tensor(xs[:, t, :], row, tokf[:, t:t + 1], xs[:, t, :], ALU.mult, ALU.add)
                ins.then_inc(s_add, 1)
                vec.wait_ge(s_add, g + 1)
                for t in range(G):
                    ins = vec.bn_stats(bst[:, t, :], xs[:, g * G + t, :])
                ins.then_inc(s_stat, 1)
                vec.wait_ge(s_stat, g + 1)
                for t in range(G):
                    ins = vec.bn_aggr(mv[:, g * G + t, :], bst[:, t, :])
                ins.then_inc(s_agg, 1)

            def inverse_std(b):
                var = mv[:, b * TB:(b + 1) * TB, 1]
                vec.wait_ge(s_act, act_at(b, "std"))
                vec.reciprocal(rn[:, 1, :], rn[:, 0, :]).then_inc(s_dve, 1)
                vec.wait_ge(s_dve, dve(b, "std_rcp"))
                vec.tensor_tensor(rn[:, 2, :], rn[:, 1, :], rn[:, 1, :], ALU.mult).then_inc(s_dve, 1)
                vec.wait_ge(s_dve, dve(b, "square"))
                vec.scalar_tensor_tensor(rn[:, 2, :], var, EPS, rn[:, 2, :], ALU.add, ALU.mult).then_inc(s_dve, 1)
                vec.wait_ge(s_dve, dve(b, "times_var"))
                vec.tensor_scalar(rn[:, 2, :], rn[:, 2, :], -0.5, 1.5, ALU.mult, ALU.add).then_inc(s_dve, 1)
                vec.wait_ge(s_dve, dve(b, "newton"))
                vec.tensor_tensor(rstd[:, b * TB:(b + 1) * TB], rn[:, 1, :], rn[:, 2, :], ALU.mult).then_inc(s_dve, 1)
                vec.wait_ge(s_dve, dve(b, "rstd"))

            vec.wait_ge(s_pe, 1)
            dots(banks[0][:, 0:C], agentf, 0, s_ag)
            tok_shift(0)
            dots(banks[0][:, 0:C], agentf, 1, s_ag, (0,))
            spread_sums(0)
            dots(banks[0][:, 0:C], agentf, 1, s_ag, (1,))
            tok_shift(1)
            channel_max(0)
            for b in range(B):
                vec.wait_ge(s_act, act_at(b, "tok_exp"))
                vec.reciprocal(tok2[:, b, :], tok[:, b, :]).then_inc(s_dve, 1)
            for b in range(B):
                vec.wait_ge(s_dve, dve(b, "tok_rcp"))
                vec.tensor_tensor(tok[:, b, :], tok[:, b, :], tok2[:, b, :], ALU.mult).then_inc(s_dve, 1)
            channel_softmax(0)
            spread_column(0)
            vec.wait_ge(s_gate, 16)
            vec.tensor_copy(gate[:, :, 0, :], gatef[:]).then_inc(s_gset, 1)
            vec.wait_ge(s_gset, 1)
            vec.tensor_tensor(gate[:, :, 1, :], gatef[:], gate[:, :, 0, :].bitcast(F32), ALU.subtract).then_inc(s_gset, 1)
            token_logits(0)
            spread_sums(1)
            channel_max(1)
            channel_softmax(1)
            spread_column(1)
            token_logits(1)
            spread_value(0, wide[:, 1])
            vec.wait_ge(s_pe, pe_at(0, "value"))
            for g in range(NP):
                add_attention(g, banks[6][:, 0:C])
            inverse_std(0)
            vec.wait_ge(s_set, 1)

            def normalise(n, par):
                tile = (n - 1) * G if isinstance(n, int) else vec.snap((n - 1) * G)
                if later(n, 2):
                    vec.wait_ge(s_sc[par], (n - 1 - par) * (16 * K * G // 2))
                for t in range(G):
                    ins = vec.tensor_scalar(x2[par][:, t:t + 1, 0:C], xs[:, sl(tile + t), :], mvf[:, sl(2 * (tile + t))],
                                            rstd[:, sl(tile + t)], ALU.subtract, ALU.mult)
                ins.then_inc(s_x2, 1)

            def rows_lo(n):
                for k in range(KC):
                    vec.wait_ge(s_xhi, nth(n, KC, k))
                    ins = vec.tensor_tensor(xtlo[:, k, :], banks[k][:], xthi[:, k, :].bitcast(F32), ALU.subtract)
                ins.then_inc(s_xt, 1)

            def route(n, tile, par):
                vec.wait_ge(s_lg, n)
                vec.tensor_reduce(rt[:, 0], banks[2][:, 0:2 * G * E].rearrange("p (t h e) -> p t e h", t=G, h=2), AX.X,
                                  ALU.add).then_inc(s_lsum, 1)
                vec.wait_ge(s_lsum, n)
                vec.tensor_reduce(r4[:, 0], rt[:, 0], AX.X, ALU.max).then_inc(s_lmax, 1)
                vec.wait_ge(s_lmax, n)
                vec.tensor_tensor(rt[:, 1], rt[:, 0], r4[:, 0].unsqueeze(2).broadcast_to([P, G, E]),
                                  ALU.subtract).then_inc(s_sh, 1)
                vec.wait_ge(s_ex, n)
                vec.tensor_reduce(r4[:, 1], rt[:, 2], AX.X, ALU.add).then_inc(s_esum, 1)
                vec.wait_ge(s_esum, n)
                vec.reciprocal(r4[:, 2], r4[:, 1]).then_inc(s_rcp, 1)
                vec.wait_ge(s_rcp, n)
                vec.tensor_tensor(rt[:, 3], rt[:, 2], r4[:, 2].unsqueeze(2).broadcast_to([P, G, E]),
                                  ALU.mult).then_inc(s_score, 1)
                vec.wait_ge(s_score, n)
                vec.sem_inc(s_tick, 1)
                for t in range(G):
                    ins = vec.max(m8[:, t, :], rt[:, 3, t, :])
                ins.then_inc(s_top8, 1)
                vec.wait_ge(s_top8, n)
                vec.sem_inc(s_tick, 1)
                for t in range(G):
                    ins = vec.max_index(i8[:, t, :], m8[:, t, :], rt[:, 3, t, :])
                ins.then_inc(s_idx, 1)
                vec.tensor_copy(top[:, sl(tile, G), :], m8[:, :, 0:K])
                vec.wait_ge(s_idx, n)
                for k in range(K):
                    ins = vec.tensor_tensor(rt[:, 5 + k], eota[:].unsqueeze(1).broadcast_to([P, G, E]),
                                            i8[:, :, k:k + 1].broadcast_to([P, G, E]), ALU.is_equal)
                ins.then_inc(s_sel, 1)
                vec.tensor_copy(x2[par][:, :, C + 1:CX], i8[:, :, 1:2])
                vec.tensor_copy(x2[par][:, :, C:C + 1], twice[:, sl(tile, G)].unsqueeze(2))
                vec.wait_ge(s_sel, n)
                vec.tensor_tensor(rt[:, 7], rt[:, 5], rt[:, 6], ALU.add).then_inc(s_m, 1)

            def slots(n, tile):
                vec.wait_ge(s_pos, n)
                vec.tensor_tensor(rt[:, 8], banks[2][:, 64:64 + G * E].rearrange("p (t e) -> p t e", t=G),
                                  ebase[:].unsqueeze(1).broadcast_to([P, G, E]), ALU.add).then_inc(s_place, 1)
                vec.tensor_reduce(rt[:, 4, 0, :], rt[:, 7].rearrange("p t e -> p e t"), AX.X, ALU.add)
                vec.wait_ge(s_place, n)
                for k in range(K):
                    ins = vec.tensor_tensor(rt[:, 5 + k], rt[:, 5 + k], rt[:, 8], ALU.mult)
                ins.then_inc(s_tmp, 1)
                vec.wait_ge(s_tmp, n)
                vec.tensor_tensor(seen[:], seen[:], rt[:, 4, 0, :], ALU.add)
                for k in range(K):
                    with nc.allow_low_precision(reason="row numbers below 2**24: exact"):
                        ins = vec.tensor_reduce(slot[:, sl(tile, G), k:k + 1], rt[:, 5 + k], AX.X, ALU.add)
                ins.then_inc(s_slot, 1)

            steps = [0]

            def table(ins):
                steps[0] += 1
                ins.then_inc(s_tb, 1)
                vec.wait_ge(s_tb, steps[0])

            count, nblk, last, unit = (tc[:, n, :] for n in range(4))
            bid, start = te[:, 0, :], te[:, 1, :]
            space = stage[:, 1, :]
            grid = [space[:, n * NBK * E:(n + 1) * NBK * E].rearrange("p (j e) -> p j e", e=E) for n in range(2)]
            over = space[:, 2 * NBK * E:2 * NBK * E + E * NT].rearrange("p (e t) -> p e t", e=E)

            def block_table():
                vec.wait_ge(s_cnt, 1)
                vec.wait_ge(s_wlo, SPLIT[4])
                vec.memset(unit, 1.0)
                table(vec.tensor_copy(count, banks[2][:, 128:128 + E]))
                vec.tensor_tensor(zrow[:], count[0:1, :], ebase[0:1, :], ALU.add).then_inc(s_ends, 1)
                table(vec.tensor_tensor(over, thr[:].unsqueeze(1).broadcast_to([P, E, NT]),
                                        count.unsqueeze(2).broadcast_to([P, E, NT]), ALU.is_lt))
                table(vec.tensor_reduce(nblk, over, AX.X, ALU.add))
                table(vec.tensor_tensor_scan(last, unit, nblk, 0.0, ALU.mult, ALU.add))
                table(vec.tensor_tensor(grid[0], jota[:].unsqueeze(2).broadcast_to([P, NBK, E]),
                                        last.unsqueeze(1).broadcast_to([P, NBK, E]), ALU.is_ge))
                table(vec.tensor_tensor(grid[1], grid[0], nblk.unsqueeze(1).broadcast_to([P, NBK, E]), ALU.mult))
                vec.tensor_reduce(bid, grid[0], AX.X, ALU.add)
                table(vec.tensor_reduce(start, grid[1], AX.X, ALU.add))
                vec.tensor_scalar(bexpf[:], bid, float(E - 1), None, ALU.min)
                vec.tensor_scalar(bexp[:], bid[0:1], float(E - 1), None, ALU.min)
                table(vec.tensor_tensor(start, jota[:], start, ALU.subtract))
                table(vec.tensor_scalar(bid, bid, float(CAP), None, ALU.mult))
                table(vec.scalar_tensor_tensor(brow[:], start[0:1], float(P), bid[0:1], ALU.mult, ALU.add))
                vec.engine_nop().then_inc(s_tbl, 1)
                near = [bexpf[0:1, o:o + NBK - 4].rearrange("o (q f) -> o q f", f=4)[:, :, f]
                        for o, f in ((0, 2), (0, 3), (4, 0), (4, 1), (4, 2), (4, 3))]
                table(vec.tensor_copy(pack[:], near[5]))
                for k in (4, 3, 2, 1):
                    table(vec.scalar_tensor_tensor(pack[:], pack[:], float(E), near[k], ALU.mult, ALU.add))
                vec.scalar_tensor_tensor(packed[:], pack[:], float(E), near[0], ALU.mult, ALU.add).then_inc(s_pack, 1)

            def group(n, par):
                tile = (n - 1) * G if isinstance(n, int) else vec.snap((n - 1) * G)
                route(n, tile, par)
                for m in range(MC):
                    buf = (par + m) % 2
                    if m == 2 and not more(n):
                        slots(n, tile)
                    vec.wait_ge(s_sg[m], n)
                    vec.tensor_tensor(prod[buf], banks[4 + 2 * buf][:], sg[buf], ALU.mult).then_inc(s_pr[m], 1)
                    vec.wait_ge(s_hhi[m], n)
                    vec.tensor_tensor(htlo[:, m, :], prod[buf], hthi[:, m, :].bitcast(F32), ALU.subtract).then_inc(s_ht, 1)
                    if m == 1 and more(n):
                        if isinstance(n, int) and n == 1:
                            vec.wait_ge(s_pe, pe_at(1, "value"))
                        normalise(n + 1, 1 - par)
                if more(n):
                    slots(n, tile)
                    rows_lo(n + 1)
                else:
                    block_table()
                for u, bank in enumerate((banks[4 + 2 * (1 - par)], banks[3])):
                    if isinstance(n, int) and n <= 2:
                        vec.wait_ge(s_act, act_at(1, "value"))
                        add_attention(NP + 2 * (n - 1) + u, att[:])
                    vec.wait_ge(s_z[u], n)
                    vec.tensor_tensor(xs[:, sl(tile + 2 * u, 2), :], bank[:].rearrange("p (t c) -> p t c", t=2),
                                      x2[par][:, 2 * u:2 * u + 2, 0:C], ALU.add).then_inc(s_zev[u], 1)
                if isinstance(n, int) and n == 2:
                    inverse_std(1)

            normalise(1, 0)
            spread_value(1, junk[:, G - 1])
            rows_lo(1)
            groups(vec, group)

            def step(at):
                if rows := at(1):
                    c, par, _, _ = rows
                    vec.wait_ge(s_bxhi[par], c)
                    vec.tensor_tensor(bxlo[par][:].rearrange("p k t -> p (k t)"), bank_x[par][:, 0:C],
                                      bxhi[par][:].rearrange("p k t -> p (k t)").bitcast(F32),
                                      ALU.subtract).then_inc(s_bx[par], 1)
                if now := at(0):
                    c, par, _, _ = now
                    vec.wait_ge(s_bsg[par], c)
                    vec.tensor_tensor(bprod[par][:, 0:H], bank_h[par][:, 0:H], bsg[par], ALU.mult)
                    vec.tensor_tensor(bprod[par][:, H:2 * P], bank_h[par][:, P:H], bsg[par][:, P:H],
                                      ALU.mult).then_inc(s_bpr[par], 1)
                if hidden := at(-1):
                    c, par, _, _ = hidden
                    vec.wait_ge(s_bhhi[par], c)
                    vec.tensor_tensor(bhlo[par][:], bank_t[par][:, 0:P], bhhi[par][:, 0, :].bitcast(F32), ALU.subtract)
                    vec.tensor_tensor(bhhi[par][HR:P, 1, :], bank_t[par][HR:P, P:2 * P],
                                      bhhi[par][HR:P, 1, :].bitcast(F32), ALU.subtract).then_inc(s_bht[par], 1)

            blocks(vec, step)

            def sums(q):
                vec.wait_ge(s_first, q + 1)
                for t in range(G):
                    z = xs[:, q * G + t, :]
                    ins = vec.scalar_tensor_tensor(z, got[q][:, t, 1, :], top[:, q * G + t, 1:2], z, ALU.mult, ALU.add)
                ins.then_inc(s_sum, 1)
                vec.wait_ge(s_sum, q + 1)
                for t in range(G):
                    ins = vec.bn_stats(bst[:, t, :], xs[:, q * G + t, :])
                ins.then_inc(s_bst, 1)
                vec.wait_ge(s_bst, q + 1)
                for t in range(G):
                    ins = vec.bn_aggr(mv[:, q * G + t, :], bst[:, t, :])
                ins.then_inc(s_var, 1)

            def scale_and_shift(u):
                start, size = UNITS[u]
                tiles = slice(start * G, (start + size) * G)
                mean, var = mv[:, tiles, 0], mv[:, tiles, 1]
                std, rough, work, fine, shift = (a[:, tiles] for a in ln2)
                vec.wait_ge(s_std, u + 1)
                vec.reciprocal(rough, std).then_inc(s_n[0], 1)
                vec.wait_ge(s_n[0], u + 1)
                vec.tensor_tensor(work, rough, rough, ALU.mult).then_inc(s_n[1], 1)
                vec.wait_ge(s_n[1], u + 1)
                vec.scalar_tensor_tensor(work, var, EPS, work, ALU.add, ALU.mult).then_inc(s_n[2], 1)
                vec.wait_ge(s_n[2], u + 1)
                vec.tensor_scalar(work, work, -0.5, 1.5, ALU.mult, ALU.add).then_inc(s_n[3], 1)
                vec.wait_ge(s_n[3], u + 1)
                vec.tensor_tensor(fine, rough, work, ALU.mult).then_inc(s_n[4], 1)
                vec.wait_ge(s_n[4], u + 1)
                vec.scalar_tensor_tensor(shift, mean, -1.0, fine, ALU.mult, ALU.mult).then_inc(s_shift, 1)

            for q in range(UNITS[0][1]):
                sums(q)
            for u, (start, size) in enumerate(UNITS):
                behind = start + size
                if behind < NG:
                    sums(behind)
                scale_and_shift(u)
                if u + 1 < len(UNITS):
                    for q in range(behind + 1, behind + UNITS[u + 1][1]):
                        sums(q)


def kernel(**inputs):
    import concourse.bacc as bacc
    from concourse.bass_utils import run_bass_kernel_spmd

    def laid(a, *axes):
        return np.ascontiguousarray(np.transpose(inputs[a], axes) if axes else inputs[a])

    nc = bacc.Bacc("TRN2", target_bir_lowering=False, num_devices=1)
    arrays = {
        "x": laid("L0_attn_x"),
        "w_qkv": laid("L0_attn_w_qkv"),
        "w_kv_t": np.ascontiguousarray(np.transpose(inputs["L0_attn_w_qkv"])[:, C:]),
        "w_conv": np.ascontiguousarray(np.reshape(inputs["L0_attn_w_conv1"], (KC, P)).T),
        "gate_t": laid("L0_ffn_gate_w", 1, 0),
        "w1_t": laid("L0_ffn_W1", 0, 2, 1),
        "w2_t": laid("L0_ffn_W2", 0, 2, 1),
        "ws1_t": laid("L0_ffn_Ws1", 1, 0),
        "ws2_t": laid("L0_ffn_Ws2", 1, 0),
    }
    args = [nc.dram_tensor(n, a.shape, mybir.dt.from_np(a.dtype), kind="ExternalInput").ap() for n, a in arrays.items()]
    out = nc.dram_tensor("out", (B, N, C), F32, kind="ExternalOutput").ap()
    post_norm_layer(nc, *args, out)
    r = run_bass_kernel_spmd(nc, [arrays], core_ids=[0])
    return r.results[0]["out"]
```
